# Optimizing a Trainium2 kernel written in Bass

```python
import numpy as np
import jax
import jax.numpy as jnp

def _softmax(x, axis=-1):
    return jax.nn.softmax(x, axis=axis)

def _gelu(x):
    return jax.nn.gelu(x, approximate=True)

def _silu(x):
    return jax.nn.silu(x)

def _sigmoid(x):
    return jax.nn.sigmoid(x)

def _layernorm(x, axis=-1, eps=1e-05):
    m = jnp.mean(x, axis=axis, keepdims=True)
    v = jnp.var(x, axis=axis, keepdims=True)
    return (x - m) / jnp.sqrt(v + eps)

def _scatter_add(tgt, idx, src, axis=0):
    return tgt.at[idx].add(src)

def _segment_sum(src, seg, n):
    return jax.ops.segment_sum(src, seg, n)
kernel_name = 'mk_recurrent_d1_jaxref_r8_1d55e1'

def setup_inputs(seed: int=0):
    np.random.seed(seed)
    _w = jnp.asarray

    def _L0_attn_setup():
        import jax, jax.numpy as jnp
        import numpy as np
        B, L, D, H = (2, 256, 128, 16)
        Dh = D // H
        key = jax.random.key(seed)
        kx, kq, kk, kv, ko = jax.random.split(key, 5)
        scale = 1.0 / np.sqrt(D)
        return {'x': jax.random.normal(kx, (B, L, D), dtype=jnp.float32), 'Wq': jax.random.normal(kq, (D, H, Dh), dtype=jnp.float32) * scale, 'Wk': jax.random.normal(kk, (D, H, Dh), dtype=jnp.float32) * scale, 'Wv': jax.random.normal(kv, (D, H, Dh), dtype=jnp.float32) * scale, 'Wout': jax.random.normal(ko, (H, Dh, D), dtype=jnp.float32) * (1.0 / np.sqrt(D))}
    _L0_attn_in = _L0_attn_setup()

    def _L0_ffn_setup():
        import jax, jax.numpy as jnp
        import numpy as np
        DIM = 128
        HIDDEN = 384
        SCALE = 1.0 / 127.0

        def _dequant(w_int, dtype):
            return w_int.astype(dtype) * jnp.asarray(SCALE, dtype)
        key = jax.random.key(seed)
        k_x, k_g, k_u, k_d = jax.random.split(key, 4)
        x = jax.random.normal(k_x, (4, 256, DIM), dtype=jnp.float32)
        w_gate = jax.random.randint(k_g, (HIDDEN, DIM), -127, 128, dtype=jnp.int32)
        w_up = jax.random.randint(k_u, (HIDDEN, DIM), -127, 128, dtype=jnp.int32)
        w_down = jax.random.randint(k_d, (DIM, HIDDEN), -127, 128, dtype=jnp.int32)
        return {'x': x, 'w_gate': w_gate, 'w_up': w_up, 'w_down': w_down}
    _L0_ffn_in = _L0_ffn_setup()
    _d = {'L0_attn_x': _L0_attn_in['x'], 'L0_attn_Wq': _L0_attn_in['Wq'], 'L0_attn_Wk': _L0_attn_in['Wk'], 'L0_attn_Wv': _L0_attn_in['Wv'], 'L0_attn_Wout': _L0_attn_in['Wout'], 'L0_ffn_w_gate': _L0_ffn_in['w_gate'], 'L0_ffn_w_up': _L0_ffn_in['w_up'], 'L0_ffn_w_down': _L0_ffn_in['w_down']}
    _x0 = _d['L0_attn_x']
    _d['L0_attn_x'] = jax.random.normal(jax.random.fold_in(jax.random.key(seed), 1), (16, 512, 128), dtype=_x0.dtype)
    del _x0
    return _d

def reference(L0_attn_x, L0_attn_Wq, L0_attn_Wk, L0_attn_Wv, L0_attn_Wout, L0_ffn_w_gate, L0_ffn_w_up, L0_ffn_w_down):

    def _L0_attn_ref(x, Wq, Wk, Wv, Wout):
        import jax, jax.numpy as jnp
        import numpy as np
        B, L, D, H = (2, 256, 128, 16)
        Dh = D // H
        q = jnp.einsum('bld,dhe->blhe', x, Wq)
        k = jnp.einsum('bld,dhe->blhe', x, Wk)
        v = jnp.einsum('bld,dhe->blhe', x, Wv)
        a = jnp.einsum('bqhd,bkhd->bhqk', q, k) / Dh ** 0.5
        Lq = x.shape[1]
        mask = jnp.tril(jnp.ones((1, 1, Lq, Lq), dtype=jnp.bool_))
        NEG_INF = jnp.finfo(jnp.float32).min
        a = jnp.where(mask, a, NEG_INF)
        a = jax.nn.softmax(a, axis=-1)
        o = jnp.einsum('bhqk,bkhd->bqhd', a, v)
        return jnp.einsum('blhe,hed->bld', o, Wout)

    def _L0_ffn_ref(x, w_gate, w_up, w_down):
        import jax, jax.numpy as jnp
        import numpy as np
        DIM = 128
        HIDDEN = 384
        SCALE = 1.0 / 127.0

        def _dequant(w_int, dtype):
            return w_int.astype(dtype) * jnp.asarray(SCALE, dtype)
        wg = _dequant(w_gate, x.dtype)
        wu = _dequant(w_up, x.dtype)
        wd = _dequant(w_down, x.dtype)
        gate = jnp.einsum('bsd,hd->bsh', x, wg)
        up = jnp.einsum('bsd,hd->bsh', x, wu)
        h = jax.nn.silu(gate) * up
        return jnp.einsum('bsh,dh->bsd', h, wd)
    x = L0_attn_x
    xn = _layernorm(x, axis=-1)
    s = _L0_attn_ref(xn, L0_attn_Wq, L0_attn_Wk, L0_attn_Wv, L0_attn_Wout)
    g = _silu(_L0_ffn_ref(xn, L0_ffn_w_gate, L0_ffn_w_up, L0_ffn_w_down))
    x = x + s * g
    return x

_drawn_inputs = setup_inputs


def setup_inputs(seed=0):
    import zlib

    import numpy as np

    out = dict(_drawn_inputs(seed))
    spreads = {}
    factors = {}
    for name, (base, spread) in spreads.items():
        noise = np.random.default_rng([zlib.crc32(name.encode()), seed]).standard_normal(out[name].shape)
        drawn = base * np.exp(spread * noise) if base else spread * noise
        out[name] = jnp.asarray(drawn.astype(out[name].dtype))
    for name, factor in factors.items():
        out[name] = (out[name] * factor).astype(out[name].dtype)
    return out
```

```python
from contextlib import ExitStack

import concourse.bass as bass
from concourse import mybir

F32 = mybir.dt.float32
BF16 = mybir.dt.bfloat16
I32 = mybir.dt.int32
ACT = mybir.ActivationFunctionType
ALU = mybir.AluOpType
AX = mybir.AxisListType

B, L, D, H = 16, 512, 128, 16
E = D // H
HID = 384
T = L // 128
HC = HID // 128
TERMS = 6
Q_PART = [0, 0, 0, 1, 1, 2]
K_PART = [0, 1, 2, 0, 1, 0]
KQ = TERMS * E
KM = KQ + 2
SL = H // 2
NBUF = 3
RING = 3
U1, U2 = 44, 40
SLOTS = 20
NEWTON = 14
MASKED = -3.0e38
SCALE = 1.0 / 127.0
EPS = 1e-5
LOOP0, LOOP1 = 2, 14


class Batch:

    def __init__(self, k, off):
        self.k, self.off, self.buf = k, off, off % NBUF
        self.looped = not isinstance(k, int)

    def at(self, d):
        return Batch(self.k, self.off + d)

    @property
    def n(self):
        return self.k * NBUF + self.off if self.looped else self.off

    @property
    def real(self):
        return self.looped or 0 <= self.off < B

    def after(self, n):
        return self.looped or self.off >= n

    def count(self, per_batch, j):
        if self.looped:
            assert self.off * per_batch + j > 0
            return self.k * (NBUF * per_batch) + (self.off * per_batch + j)
        return self.off * per_batch + j

    def turns(self, j):
        if self.looped:
            assert self.off // NBUF + j > 0
            return self.k * 16 + 16 * (self.off // NBUF + j)
        return 16 * (self.off // NBUF + j)


def alone(eng, consts, value):
    if not isinstance(value, int):
        eng.lower_val(value)
        eng.wait_ge(consts, 1)
    return value


def first_pass_units(half):
    s0 = 4 * half
    pairs = [(3, [s0 + x]) for x in range(4)] + [(2, [s0 + x]) for x in range(4)]
    pairs += [(1, [s0, s0 + 1]), (1, [s0 + 2, s0 + 3]), (0, [s0 + x for x in range(4)])]
    return pairs


P1_SLOT = []
for _s in range(SLOTS):
    _h, _x = divmod(_s, 10)
    _p = _x if _x <= 4 else _x + 1
    P1_SLOT.append([11 * _h + _p] + ([11 * _h + 5] if _x == 4 else []))
P1_PAIRS = first_pass_units(0) + first_pass_units(1)

PV_SLOT = {6: (0, 0), 7: (0, 1), 8: (0, 2), 9: (0, 3), 10: (1, 0), 11: (1, 1), 12: (1, 2), 13: (1, 3),
           15: (2, 0), 16: (2, 1), 17: (2, 2), 18: (2, 3), 0: (3, 0), 1: (3, 1), 2: (3, 2), 3: (3, 3)}


def build(nc, x, wq, wk, wv, wout, wg, wu, wd, out):
    ctx = ExitStack()
    with ctx:
        def sb(name, shape, dt):
            return ctx.enter_context(nc.sbuf_tensor(name, shape, dt))

        def pb(name, shape):
            return ctx.enter_context(nc.psum_tensor(name, shape, F32))

        def sem(name):
            return ctx.enter_context(nc.semaphore(name))

        wq_nat, wk_nat = sb("wq_nat", [128, D], F32), sb("wk_nat", [128, D], F32)
        wq_sb, wk_sb = sb("wq_sb", [128, D], F32), sb("wk_sb", [128, D], F32)
        wv_sb = sb("wv_sb", [128, D], F32)
        wo_nat, wo_sb = sb("wo_nat", [128, D], F32), sb("wo_sb", [128, D], F32)
        wg_int, wu_int = sb("wg_int", [128, HC, D], I32), sb("wu_int", [128, HC, D], I32)
        wd_int = sb("wd_int", [128, HID], I32)
        wg_f, wu_f = sb("wg_f", [128, HC, D], F32), sb("wu_f", [128, HC, D], F32)
        wd_f = sb("wd_f", [128, HID], F32)
        wgT, wuT, wdT = (sb(n, [128, HC, 128], F32) for n in ("wgT", "wuT", "wdT"))
        ident = sb("ident", [128, 128], F32)
        ident_b = sb("ident_b", [128, 128], BF16)
        shifted = sb("shifted", [128, 192], BF16)
        causal = sb("causal", [128, 128], BF16)
        x_nat = [sb(f"x_nat{n}", [128, T, D], F32) for n in range(NBUF)]
        x_res = [sb(f"x_res{n}", [128, T, D], F32) for n in range(NBUF)]
        stats = sb("stats", [128, T, 6], F32)
        moments = sb("moments", [128, T, 2], F32)
        var_e, rstd, newt = sb("var_e", [128, T], F32), sb("rstd", [128, T], F32), sb("newt", [128, T], F32)
        x_hat = sb("x_hat", [128, T, D], F32)
        xT = [sb(f"xT{n}", [128, L], F32) for n in range(NBUF)]
        q_parts, k_parts = sb("q_parts", [128, 3, L], BF16), sb("k_parts", [128, 3, L], BF16)
        q_rest, k_rest = sb("q_rest", [128, L], F32), sb("k_rest", [128, L], F32)
        q_stack = [sb(f"q_stack{n}", [128, SL, L], BF16) for n in range(NBUF)]
        k_stack = [sb(f"k_stack{n}", [128, SL, L], BF16) for n in range(NBUF)]
        v_cols = [sb(f"v_cols{n}", [128, T, 2, 2, 4, 32], F32) for n in range(NBUF)]
        negmax = sb("negmax", [128, 2, T, 2, 4], F32)
        negmax_p = sb("negmax_p", [128, 2, T, 2, 8], BF16)
        mT_sb = sb("mT_sb", [16, 2, L], BF16)
        probs = [sb(f"probs{n}", [128, 10, L], F32) for n in range(2)]
        o_ev = sb("o_ev", [128, 2, L], F32)
        o_sb, den_sb, rden, o_norm = (sb(n, [128, L], F32) for n in ("o_sb", "den_sb", "rden", "o_norm"))
        tanh_g, gate_s = sb("tanh_g", [128, L], F32), sb("gate_s", [128, L], F32)
        hT = sb("hT", [128, HC, L], F32)
        tanh_f = sb("tanh_f", [128, L], F32)
        g_out = [sb(f"g_out{n}", [128, L], F32) for n in range(NBUF)]
        sg = sb("sg", [128, L], F32)
        y_sb = [sb(f"y_sb{n}", [128, L], F32) for n in range(NBUF)]
        s1 = [pb(f"s1_{n}", [128, 512]) for n in range(RING)]
        s2 = [pb(f"s2_{n}", [128, 512]) for n in range(RING)]
        ov = pb("ov", [128, 512])
        mb = pb("mb", [128, 512])

        w_attn, w_ffn = sem("w_attn"), sem("w_ffn")
        w_conv, w_tr, w_ready = sem("w_conv"), sem("w_tr"), sem("w_ready")
        consts = sem("consts")
        x_in = [sem(f"x_in{n}") for n in range(NBUF)]
        xr_in = [sem(f"xr_in{n}") for n in range(NBUF)]
        ln_stats = sem("ln_stats")
        newton = sem("newton")
        xhat_ready = sem("xhat_ready")
        xT_full, xT_out = sem("xT_full"), sem("xT_out")
        q_full, q_hi, q_r1, q_mid, q_lo = (sem(n) for n in ("q_full", "q_hi", "q_r1", "q_mid", "q_lo"))
        k_full, k_hi, k_r1, k_mid, k_lo = (sem(n) for n in ("k_full", "k_hi", "k_r1", "k_mid", "k_lo"))
        stack_in = sem("stack_in")
        v_full, v_out = sem("v_full"), sem("v_out")
        gate_full, tanh_done, gs_done = sem("gate_full"), sem("tanh_done"), sem("gs_done")
        up_full, h_done = sem("up_full"), sem("h_done")
        down_full, tf_done, g_done = sem("down_full"), sem("tf_done"), sem("g_done")
        s1_full, s1_red = sem("s1_full"), sem("s1_red")
        nm_ready, mT_full, mT_out = sem("nm_ready"), sem("mT_full"), sem("mT_out")
        m_in = [sem(f"m_in{n}") for n in range(2)]
        s2_full, exp_done, masked = sem("s2_full"), sem("exp_done"), sem("masked")
        pv_done, ov_out = sem("pv_done"), sem("ov_out")
        o_in = [sem(f"o_in{n}") for n in range(2)]
        rden_done, on_ready = sem("rden_done"), sem("on_ready")
        out_full, y_done, fin_done = sem("out_full"), sem("y_done"), sem("fin_done")
        stored = sem("stored")
        STACK = 16 * 4 * TERMS

        def program(eng, step):
            for i in range(-2, LOOP0):
                step(Batch(0, i))
            with eng.Fori(0, (LOOP1 - LOOP0) // NBUF) as k:
                for r in range(NBUF):
                    step(Batch(k, LOOP0 + r))
            for i in range(LOOP1, B + 1):
                step(Batch(0, i))

        def tokens(t, b):
            return t[b.n].rearrange("(t p) d -> p t d", p=128)

        block = ctx.enter_context(nc.Block())

        @block.sync
        def _(sp):
            sp.dma_start(x_nat[0][:, :, :], x[0].rearrange("(t p) d -> p t d", p=128)).then_inc(x_in[0], 16)
            sp.dma_start(wq_nat[:, :], wq.rearrange("d h e -> d (h e)")).then_inc(w_attn, 16)
            sp.dma_start(wk_nat[:, :], wk.rearrange("d h e -> d (h e)")).then_inc(w_attn, 16)
            sp.dma_start(wv_sb[:, :], wv.rearrange("d h e -> d (h e)")).then_inc(w_attn, 16)
            sp.dma_start(wo_nat[:, :], wout.rearrange("h e d -> (h e) d")).then_inc(w_attn, 16)
            sp.dma_start(wg_int[:, :, :], wg.rearrange("(c p) d -> p c d", p=128)).then_inc(w_ffn, 16)
            sp.dma_start(wu_int[:, :, :], wu.rearrange("(c p) d -> p c d", p=128)).then_inc(w_ffn, 16)
            sp.dma_start(wd_int[:, :], wd[:, :]).then_inc(w_ffn, 16)
            def spread(parts, stack, part_of, part, b):
                for side in range(2):
                    for term in range(TERMS):
                        if part_of[term] != part:
                            continue
                        row = 64 * side + E * term
                        sp.dma_start(stack[b.buf][row:row + E, :, :],
                                     parts[64 * side:64 * side + 64, part, :]).then_inc(stack_in, 16)

            def send_max(b, half):
                sp.wait_ge(mT_out, alone(sp, consts, b.count(2, half + 1)))
                pitch = SL * L
                for part in range(2):
                    dst = bass.AP(q_stack[b.buf], (KQ + part) * pitch + 4 * half * L,
                                  [[64 * pitch, 2], [L, 4], [1, L]])
                    sp.dma_start(dst, mT_sb[8 * part:8 * part + 8, half, :]).then_inc(m_in[half], 16)

            def send_o(b, half):
                sp.wait_ge(ov_out, alone(sp, consts, b.count(2, half + 1)))
                if b.after(1):
                    sp.wait_ge(on_ready, alone(sp, consts, b.count(1, 0)))
                for dst, row in ((o_sb, 0), (den_sb, 1)):
                    sp.dma_start(dst[64 * half:64 * half + 64, :], o_ev[row::2, half, :]).then_inc(o_in[half], 16)

            def step(i):
                fe, ff, tail = i.at(2), i.at(1), i.at(-1)
                if fe.real and (fe.looped or fe.off > 0):
                    if fe.after(3):
                        sp.wait_ge(xhat_ready, alone(sp, consts, fe.at(-2).count(1, 0)))
                    sp.dma_start(x_nat[fe.buf][:, :, :], tokens(x, fe)).then_inc(x_in[fe.buf], 16)
                if i.real:
                    send_max(i, 1)
                if i.real:
                    sp.dma_start(x_res[i.buf][:, :, :], tokens(x, i)).then_inc(xr_in[i.buf], 16)
                if tail.real:
                    send_o(tail, 1)
                if fe.real:
                    if fe.after(3):
                        sp.wait_ge(s2_full, alone(sp, consts, fe.at(-2).count(U2, 0)))
                    sp.wait_ge(consts, 1)
                    sp.wait_ge(q_hi, alone(sp, consts, fe.count(1, 1)))
                    spread(q_parts, q_stack, Q_PART, 0, fe)
                    sp.wait_ge(k_hi, alone(sp, consts, fe.count(1, 1)))
                    spread(k_parts, k_stack, K_PART, 0, fe)
                    sp.wait_ge(q_mid, alone(sp, consts, fe.count(1, 1)))
                    spread(q_parts, q_stack, Q_PART, 1, fe)
                    sp.wait_ge(k_mid, alone(sp, consts, fe.count(1, 1)))
                    spread(k_parts, k_stack, K_PART, 1, fe)
                    sp.wait_ge(q_lo, alone(sp, consts, fe.count(1, 1)))
                    spread(q_parts, q_stack, Q_PART, 2, fe)
                    sp.wait_ge(k_lo, alone(sp, consts, fe.count(1, 1)))
                    spread(k_parts, k_stack, K_PART, 2, fe)
                if ff.real:
                    send_max(ff, 0)
                if i.real:
                    send_o(i, 0)
                if tail.real:
                    sp.wait_ge(fin_done, alone(sp, consts, tail.count(1, 1)))
                    sp.dma_start(tokens(out, tail),
                                 y_sb[tail.buf][:, :].rearrange("p (t d) -> p t d", t=T)).then_inc(stored, 16)

            program(sp, step)
            sp.wait_ge(stored, 16 * B)

        @block.gpsimd
        def _(pool):
            nc.gpsimd.memset(ident[:, :], 1.0)
            nc.gpsimd.memset(shifted[:, :], 0.0)
            nc.gpsimd.memset(causal[:, :], MASKED).then_inc(w_conv, 1)
            pool.wait_ge(w_conv, 1)
            nc.gpsimd.affine_select(out=ident[:, :], in_=ident[:, :], compare_op=ALU.is_equal, fill=0.0,
                                    base=0, pattern=[[1, 128]], channel_multiplier=-1).then_inc(w_conv, 1)
            mid = shifted[:, 64:128]
            nc.gpsimd.affine_select(out=mid, in_=mid, compare_op=ALU.not_equal, fill=1.0,
                                    base=0, pattern=[[1, 64]], channel_multiplier=-1).then_inc(w_conv, 1)
            nc.gpsimd.affine_select(out=causal[0:64, :], in_=causal[0:64, :], compare_op=ALU.is_gt, fill=0.0,
                                    base=0, pattern=[[1, 128]], channel_multiplier=-1).then_inc(w_conv, 1)
            pool.wait_ge(w_conv, 4)
            nc.gpsimd.affine_select(out=mid, in_=mid, compare_op=ALU.not_equal, fill=1.0,
                                    base=64, pattern=[[1, 64]], channel_multiplier=-1).then_inc(w_conv, 1)
            nc.gpsimd.affine_select(out=causal[:, :], in_=causal[:, :], compare_op=ALU.is_gt, fill=0.0,
                                    base=64, pattern=[[1, 128]], channel_multiplier=-1).then_inc(w_conv, 1)

            def rsqrt(b):
                pool.wait_ge(ln_stats, alone(pool, consts, b.count(2, 2)))
                if b.after(1):
                    pool.wait_ge(xhat_ready, alone(pool, consts, b.count(1, 0)))
                nc.gpsimd.tensor_scalar(var_e[:, :], moments[:, :, 1], EPS, None, ALU.add).then_inc(newton, 1)
                pool.wait_ge(newton, alone(pool, consts, b.count(NEWTON, 1)))
                nc.gpsimd.tensor_scalar(rstd[:, :].bitcast(I32), var_e[:, :].bitcast(I32),
                                        -0.5, float(0x5F3759DF), ALU.mult, ALU.add).then_inc(newton, 1)
                for n in range(3):
                    pool.wait_ge(newton, alone(pool, consts, b.count(NEWTON, 4 * n + 2)))
                    nc.gpsimd.tensor_tensor(newt[:, :], rstd[:, :], rstd[:, :], ALU.mult).then_inc(newton, 1)
                    pool.wait_ge(newton, alone(pool, consts, b.count(NEWTON, 4 * n + 3)))
                    nc.gpsimd.tensor_tensor(newt[:, :], newt[:, :], var_e[:, :], ALU.mult).then_inc(newton, 1)
                    pool.wait_ge(newton, alone(pool, consts, b.count(NEWTON, 4 * n + 4)))
                    nc.gpsimd.tensor_scalar(newt[:, :], newt[:, :], -0.5, 1.5,
                                            ALU.mult, ALU.add).then_inc(newton, 1)
                    pool.wait_ge(newton, alone(pool, consts, b.count(NEWTON, 4 * n + 5)))
                    nc.gpsimd.tensor_tensor(rstd[:, :], rstd[:, :], newt[:, :], ALU.mult).then_inc(newton, 1)

            def mask(b, slot):
                g, r = divmod(slot, 5)
                pool.wait_ge(exp_done, alone(pool, consts, b.count(U2, 2 * slot + 2)))
                pair = probs[g % 2][:, 2 * r:2 * r + 2, :].rearrange("p u (n c) -> p u n c", c=128)
                if r < 2:
                    parts = [pair[:, :, 0, :]]
                elif r < 4:
                    parts = [pair[:, 0, 0::3, :], pair[:, 1, 0::3, :]]
                else:
                    parts = [pair[:, :, :, :].rearrange("p u n c -> p (u n) c")[:, 0::2, :]]
                for part in parts:
                    nc.gpsimd.affine_select(out=part, in_=part, compare_op=ALU.is_ge, fill=0.0, base=0,
                                            pattern=[[0, part.shape[1]], [1, 128]],
                                            channel_multiplier=-1).then_inc(masked, 1)

            def step(i):
                fe, tail = i.at(2), i.at(-1)
                for slot in range(SLOTS):
                    if i.real:
                        mask(i, slot)
                    if slot == 2 and fe.real:
                        rsqrt(fe)
                    if slot == 8 and fe.real:
                        pool.wait_ge(q_mid, alone(pool, consts, fe.count(1, 1)))
                        nc.gpsimd.tensor_tensor(q_parts[:, 2, :], q_rest[:, :], q_parts[:, 1, :],
                                                ALU.subtract).then_inc(q_lo, 1)
                    if slot == 9 and fe.real:
                        pool.wait_ge(k_mid, alone(pool, consts, fe.count(1, 1)))
                        nc.gpsimd.tensor_tensor(k_parts[:, 2, :], k_rest[:, :], k_parts[:, 1, :],
                                                ALU.subtract).then_inc(k_lo, 1)
                    if slot == 10 and tail.real:
                        pool.wait_ge(rden_done, alone(pool, consts, tail.count(1, 1)))
                        if tail.after(1):
                            pool.wait_ge(out_full, alone(pool, consts, tail.count(1, 0)))
                        nc.gpsimd.tensor_tensor(o_norm[:, :], o_sb[:, :], rden[:, :], ALU.mult).then_inc(on_ready, 1)
                    if slot == 15 and tail.real:
                        if tail.after(1):
                            pool.wait_ge(stored, alone(pool, consts, tail.count(16, 0)))
                        pool.wait_ge(xr_in[tail.buf], alone(pool, consts, tail.turns(1)))
                        pool.wait_ge(y_done, alone(pool, consts, tail.count(1, 1)))
                        nc.gpsimd.tensor_tensor(y_sb[tail.buf][:, :], sg[:, :],
                                                x_res[tail.buf][:, :, :].rearrange("p t d -> p (t d)"),
                                                ALU.add).then_inc(fin_done, 1)

            program(pool, step)

        @block.scalar
        def _(act):
            def copy(dst, src):
                return nc.scalar.activation(dst, src, ACT.Copy)

            for n, (dst, src) in enumerate(((wgT, mb), (wuT, ov), (wdT, s1[0]))):
                act.wait_ge(w_tr, n + 1)
                copy(dst[:, :, :].rearrange("p c m -> p (c m)"), src[:, 0:HID]).then_inc(w_ready, 1)

            def exp_unit(b, slot, side):
                g, r = divmod(slot, 5)
                u = 2 * slot + side
                if r == 0 and side == 0:
                    if b.after(1) or g > 1:
                        act.wait_ge(pv_done, b.count(16, 4 * (g - 1)))
                act.wait_ge(s2_full, b.count(U2, u + 1))
                nc.scalar.activation(probs[g % 2][:, 2 * r + side, :], s2[(U2 * b.off + u) % RING][:, :],
                                     ACT.Exp, scale=float(E) ** -0.5).then_inc(exp_done, 1)

            def step(i):
                fe, ff, tail = i.at(2), i.at(1), i.at(-1)
                for slot in range(SLOTS):
                    if slot == 2 and i.real:
                        max_out(i, 1)
                    if slot == 16 and ff.real:
                        max_out(ff, 0)
                    if slot == 3 and ff.real:
                        if ff.after(3):
                            act.wait_ge(pv_done, ff.at(-2).count(16, 0))
                        act.wait_ge(v_full, ff.count(1, 1))
                        dst = v_cols[ff.buf][:, :, :, :, :, :].rearrange("p t f s c m -> p (t f) s c m")
                        src = mb[:, :].rearrange("p (g c s e) -> p g s c e", c=4, s=2, e=E)
                        copy(dst[:, :, 0, :, 0:2 * E:2], src[:, :, 0])
                        copy(dst[:, :, 1, :, 2 * E:4 * E:2], src[:, :, 1]).then_inc(v_out, 1)
                    if slot == 5 and fe.real:
                        if fe.after(3):
                            act.wait_ge(up_full, fe.at(-2).count(HC, 0))
                        act.wait_ge(xT_full, fe.count(1, 1))
                        copy(xT[fe.buf][:, :], mb[:, :]).then_inc(xT_out, 1)
                    if slot == 6 and fe.real:
                        if fe.after(1):
                            act.wait_ge(stack_in, fe.count(STACK, 0))
                        act.wait_ge(q_full, fe.count(1, 1))
                        copy(q_parts[:, 0, :], mb[:, :]).then_inc(q_hi, 1)
                    if slot == 7 and fe.real:
                        act.wait_ge(k_full, fe.count(1, 1))
                        copy(k_parts[:, 0, :], mb[:, :]).then_inc(k_hi, 1)
                        act.wait_ge(q_r1, fe.count(1, 1))
                        copy(q_parts[:, 1, :], q_rest[:, :]).then_inc(q_mid, 1)
                    if slot == 8 and fe.real:
                        act.wait_ge(k_r1, fe.count(1, 1))
                        copy(k_parts[:, 1, :], k_rest[:, :]).then_inc(k_mid, 1)
                    if slot in (8, 10, 12) and ff.real:
                        c = (slot - 8) // 2
                        if ff.after(1) or c > 0:
                            act.wait_ge(gs_done, ff.count(HC, c))
                        act.wait_ge(gate_full, ff.count(HC, c + 1))
                        nc.scalar.activation(tanh_g[:, :], mb[:, :], ACT.Tanh, scale=0.5).then_inc(tanh_done, 1)
                    if slot == 15 and ff.real:
                        if ff.after(1):
                            act.wait_ge(g_done, ff.count(1, 0))
                        act.wait_ge(down_full, ff.count(1, 1))
                        nc.scalar.activation(tanh_f[:, :], mb[:, :], ACT.Tanh, scale=0.5).then_inc(tf_done, 1)
                    if slot == 4 and tail.real:
                        heads_out(tail, 1)
                    if slot == 14 and i.real:
                        heads_out(i, 0)
                    if i.real:
                        exp_unit(i, slot, 0)
                        exp_unit(i, slot, 1)

            def max_out(b, half):
                if b.after(1):
                    act.wait_ge(m_in[half], b.count(32, 0))
                act.wait_ge(mT_full, b.count(2, half + 1))
                copy(mT_sb[:, half, :], mb[0:16, :]).then_inc(mT_out, 1)

            def heads_out(b, half):
                if b.after(1):
                    act.wait_ge(o_in[half], b.count(32, 0))
                act.wait_ge(pv_done, b.count(16, 8 * half + 8))
                copy(o_ev[:, half, :], ov[:, :]).then_inc(ov_out, 1)

            program(act, step)

        @block.vector
        def _(dve):
            for n in range(NBUF):
                nc.vector.memset(v_cols[n][:, :, :, :, :, :].rearrange("p t f s c m -> p (t f s c m)"), 0.0)
                last = nc.vector.memset(k_stack[n][:, :, :].rearrange("p s l -> p (s l)"), 1.0)
            last.then_inc(consts, 1)
            dve.wait_ge(consts, 1)
            for n in range(NBUF):
                cols = v_cols[n][:, :, :, :, :, :].rearrange("p t f s c m -> p (t f) s c m")
                nc.vector.memset(cols[:, :, 0, :, 1:2 * E:2], 1.0)
                nc.vector.memset(cols[:, :, 1, :, 2 * E + 1:4 * E:2], 1.0)
            dve.wait_ge(w_conv, 6)
            nc.vector.tensor_copy(ident_b[:, :], ident[:, :]).then_inc(consts, 1)
            dve.wait_ge(w_attn, 64)
            for nat, dst in ((wq_nat, wq_sb), (wk_nat, wk_sb)):
                src = nat[:, :].rearrange("p (f d a s e) -> p f a e s d", f=2, d=2, a=2, s=2)
                to = dst[:, :].rearrange("p (a e f s d) -> p f a e s d", a=2, e=E, f=2, s=2)
                for f in range(2):
                    for a in range(2):
                        nc.vector.tensor_copy(to[:, f, a], src[:, f, a])
            nc.vector.tensor_scalar(wo_sb[:, :], wo_nat[:, :], 0.5, None, ALU.mult).then_inc(consts, 1)
            dve.wait_ge(w_ffn, 48)
            nc.vector.tensor_scalar(wg_f[:, :, :], wg_int[:, :, :], SCALE, None, ALU.mult)
            nc.vector.tensor_scalar(wu_f[:, :, :], wu_int[:, :, :], SCALE, None, ALU.mult)
            nc.vector.tensor_scalar(wd_f[:, :], wd_int[:, :], SCALE, 0.5, ALU.mult, ALU.mult).then_inc(consts, 1)

            def reduce_units(b, pair):
                tile, slots = P1_PAIRS[pair]
                half, width = pair // 11, 128 * (tile + 1)
                for side in range(2):
                    u = 2 * pair + side
                    dve.wait_ge(s1_full, b.count(U1, u + 1))
                    src = s1[(U1 * b.off + u) % RING][:, 0:width * len(slots)]
                    lo = slots[0] - 4 * half
                    nc.vector.tensor_reduce(negmax[:, half, tile, side, lo:lo + len(slots)],
                                            src.rearrange("p (n w) -> p n w", w=width), AX.X, ALU.max,
                                            negate=True).then_inc(s1_red, 1)

            def split_max(b, half):
                if b.after(1):
                    dve.wait_ge(mT_full, b.at(-1).count(2, half + 1))
                dve.wait_ge(s1_red, b.count(U1, 22 * (half + 1)))
                src = negmax[:, half].rearrange("p t a s -> p t (a s)")
                nc.vector.tensor_copy(negmax_p[:, half, :, 0, :], src).then_inc(nm_ready, 1)
                dve.wait_ge(nm_ready, b.count(4, 2 * half + 1))
                nc.vector.tensor_tensor(negmax_p[:, half, :, 1, :], src, negmax_p[:, half, :, 0, :],
                                        ALU.subtract).then_inc(nm_ready, 1)

            def step(i):
                fe, ff, tail = i.at(2), i.at(1), i.at(-1)
                for slot in range(SLOTS):
                    if slot == 2 and fe.real:
                        dve.wait_ge(x_in[fe.buf], fe.turns(1))
                        for t in range(T):
                            last = nc.vector.bn_stats(stats[:, t, :], x_nat[fe.buf][:, t, :])
                        last.then_inc(ln_stats, 1)
                        if fe.after(1):
                            dve.wait_ge(newton, fe.count(NEWTON, 0))
                        dve.wait_ge(ln_stats, alone(dve, consts, fe.count(2, 1)))
                        for t in range(T):
                            last = nc.vector.bn_aggr(moments[:, t, :], stats[:, t, :])
                        last.then_inc(ln_stats, 1)
                    if slot == 3 and fe.real:
                        if fe.after(1):
                            dve.wait_ge(xT_full, fe.count(1, 0))
                        dve.wait_ge(newton, fe.count(NEWTON, NEWTON))
                        for t in range(T):
                            last = nc.vector.tensor_scalar(x_hat[:, t, :], x_nat[fe.buf][:, t, :],
                                                           moments[:, t, 0:1], rstd[:, t:t + 1],
                                                           ALU.subtract, ALU.mult)
                        last.then_inc(xhat_ready, 1)
                    if slot == 6 and fe.real:
                        if fe.after(1):
                            dve.wait_ge(q_lo, fe.count(1, 0))
                        dve.wait_ge(q_hi, fe.count(1, 1))
                        nc.vector.tensor_tensor(q_rest[:, :], mb[:, :], q_parts[:, 0, :], ALU.subtract).then_inc(q_r1, 1)
                    if slot == 7 and fe.real:
                        if fe.after(1):
                            dve.wait_ge(k_lo, fe.count(1, 0))
                        dve.wait_ge(k_hi, fe.count(1, 1))
                        nc.vector.tensor_tensor(k_rest[:, :], mb[:, :], k_parts[:, 0, :], ALU.subtract).then_inc(k_r1, 1)
                    if slot in (8, 10, 12) and ff.real:
                        c = (slot - 8) // 2
                        if ff.after(1) or c > 0:
                            dve.wait_ge(h_done, ff.count(HC, c))
                        dve.wait_ge(tanh_done, ff.count(HC, c + 1))
                        nc.vector.scalar_tensor_tensor(gate_s[:, :], tanh_g[:, :], 1.0, mb[:, :],
                                                       ALU.add, ALU.mult).then_inc(gs_done, 1)
                    if slot in (9, 11, 13) and ff.real:
                        c = (slot - 9) // 2
                        if ff.after(1):
                            dve.wait_ge(down_full, ff.count(1, 0))
                        dve.wait_ge(gs_done, ff.count(HC, c + 1))
                        dve.wait_ge(up_full, ff.count(HC, c + 1))
                        nc.vector.tensor_tensor(hT[:, c, :], gate_s[:, :], mb[:, :], ALU.mult).then_inc(h_done, 1)
                    if slot == 9 and tail.real:
                        if tail.after(1):
                            dve.wait_ge(on_ready, tail.count(1, 0))
                        dve.wait_ge(o_in[0], tail.count(32, 32))
                        dve.wait_ge(o_in[1], tail.count(32, 32))
                        nc.vector.reciprocal(rden[:, :], den_sb[:, :]).then_inc(rden_done, 1)
                    if slot == 14 and tail.real:
                        if tail.after(1):
                            dve.wait_ge(fin_done, tail.count(1, 0))
                        dve.wait_ge(g_done, tail.count(1, 1))
                        dve.wait_ge(out_full, tail.count(1, 1))
                        nc.vector.tensor_tensor(sg[:, :], g_out[tail.buf][:, :], mb[:, :], ALU.mult).then_inc(y_done, 1)
                    if slot == 15 and ff.real:
                        dve.wait_ge(tf_done, ff.count(1, 1))
                        if ff.after(3):
                            dve.wait_ge(y_done, ff.at(-2).count(1, 0))
                        nc.vector.scalar_tensor_tensor(g_out[ff.buf][:, :], tanh_f[:, :], 1.0, mb[:, :],
                                                       ALU.add, ALU.mult).then_inc(g_done, 1)
                    if ff.real:
                        for pair in P1_SLOT[slot]:
                            reduce_units(ff, pair)
                        if slot == 9:
                            split_max(ff, 0)
                        if slot == 19:
                            split_max(ff, 1)

            program(dve, step)

        @block.tensor
        def _(pe):
            mm = nc.tensor.matmul
            pe.wait_ge(consts, 4)
            for w, bank in ((wg_f, mb), (wu_f, ov)):
                for c in range(HC):
                    last = nc.tensor.transpose(bank[:, 128 * c:128 * c + 128], w[:, c, :], ident[:, :])
                last.then_inc(w_tr, 1)
            for c in range(HC):
                last = nc.tensor.transpose(s1[0][:, 128 * c:128 * c + 128], wd_f[:, 128 * c:128 * c + 128], ident[:, :])
            last.then_inc(w_tr, 1)
            pe.wait_ge(w_ready, 3)

            def pass1(b, pair):
                tile, slots = P1_PAIRS[pair]
                width = 128 * (tile + 1)
                if pair == 0:
                    pe.wait_ge(stack_in, b.count(STACK, STACK))
                banks = []
                for side in range(2):
                    u = 2 * pair + side
                    if b.after(1) or u >= RING:
                        pe.wait_ge(s1_red, b.count(U1, u + 1 - RING))
                    banks.append(s1[(U1 * b.off + u) % RING])
                    rows = slice(64 * side, 64 * side + KQ)
                    for n, s in enumerate(slots):
                        mm(banks[side][:, n * width:(n + 1) * width],
                           q_stack[b.buf][rows, s, 128 * tile:128 * tile + 128],
                           k_stack[b.buf][rows, s, 0:width], start=n == 0, stop=False, skip_group_check=True)
                n = len(slots)
                for side in range(2):
                    rows = slice(64 * side, 64 * side + 64)
                    diag = banks[side][:, 0:n * width].rearrange("p (n w) -> p n w", w=width)[:, :, 128 * tile:]
                    mask = causal[rows, :].unsqueeze(1).to_broadcast([64, n, 128])
                    mm(diag, shifted[rows, 64:192], mask, start=False, stop=False, skip_group_check=True)
                for side in range(2):
                    rows = slice(64 * side, 64 * side + 64)
                    diag = banks[side][:, 0:n * width].rearrange("p (n w) -> p n w", w=width)[:, :, 128 * tile + 64:]
                    mask = causal[rows, 0:64].unsqueeze(1).to_broadcast([64, n, 64])
                    mm(diag, shifted[rows, 0:128], mask, start=False, stop=True,
                       skip_group_check=True).then_inc(s1_full, 1)

            def pass2(b, slot):
                g, r = divmod(slot, 5)
                if slot in (0, 10):
                    pe.wait_ge(m_in[slot // 10], b.count(32, 32))
                jobs = {0: [(2 * g, 0, 0)], 1: [(2 * g + 1, 0, 0)],
                        2: [(2 * g, 1, 0), (2 * g, 3, 384)], 3: [(2 * g + 1, 1, 0), (2 * g + 1, 3, 384)],
                        4: [(2 * g, 2, 0), (2 * g + 1, 2, 256)]}[r]
                for n, (s, j, col) in enumerate(jobs):
                    for side in range(2):
                        u = 2 * slot + side
                        if n == 0:
                            if b.after(1) or u >= RING:
                                pe.wait_ge(exp_done, b.count(U2, u + 1 - RING))
                        rows = slice(64 * side, 64 * side + KM)
                        last = mm(s2[(U2 * b.off + u) % RING][:, col:col + L - 128 * j],
                                  k_stack[b.buf][rows, s, 128 * j:128 * j + 128],
                                  q_stack[b.buf][rows, s, 128 * j:L], start=True, stop=True)
                        if n == len(jobs) - 1:
                            last.then_inc(s2_full, 1)

            def attend(b, g, j):
                half, sub = divmod(g, 2)
                if g == 0 and j == 0:
                    pe.wait_ge(v_out, b.count(1, 1))
                if sub == 0 and j == 0:
                    if b.after(1) or half > 0:
                        pe.wait_ge(ov_out, b.count(2, half))
                pe.wait_ge(masked, b.count(28, 7 * g + (2, 6, 7, 7)[j]))
                for c in range(4):
                    side, d = c % 2, c // 2
                    unit, col = {0: (d, 0), 1: (2 + d, 0), 2: (4, 256 * d), 3: (2 + d, 384)}[j]
                    last = mm(ov[32 * c:32 * c + 32, 128 * j:L], v_cols[b.buf][:, j, half, sub, c, :],
                              probs[g % 2][:, 2 * unit + side, col:col + L - 128 * j],
                              start=sub == 0 and j == 0, stop=sub == 1 and j == 3, skip_group_check=True)
                last.then_inc(pv_done, 1)

            def max_T(b, half):
                pe.wait_ge(nm_ready, b.count(4, 2 * half + 2))
                for t in range(T):
                    last = mm(mb[0:16, 128 * t:128 * t + 128],
                              negmax_p[:, half, t].rearrange("p a h -> p (a h)"), ident_b[:, :], start=True, stop=True)
                last.then_inc(mT_full, 1)

            def step(i):
                fe, ff, tail = i.at(2), i.at(1), i.at(-1)
                for slot in range(SLOTS):
                    if ff.real:
                        for pair in P1_SLOT[slot]:
                            pass1(ff, pair)
                    if i.real:
                        pass2(i, slot)
                    if slot in PV_SLOT:
                        g, j = PV_SLOT[slot]
                        b = tail if g == 3 else i
                        if b.real:
                            attend(b, g, j)
                    if slot == 1 and i.real:
                        pe.wait_ge(mT_out, i.count(2, 1))
                        max_T(i, 1)
                    if slot == 4 and fe.real:
                        if ff.real:
                            pe.wait_ge(v_out, ff.count(1, 1))
                        pe.wait_ge(xhat_ready, fe.count(1, 1))
                        for t in range(T):
                            last = nc.tensor.transpose(mb[:, 128 * t:128 * t + 128], x_hat[:, t, :], ident[:, :])
                        last.then_inc(xT_full, 1)
                    if slot == 5 and fe.real:
                        pe.wait_ge(xT_out, fe.count(1, 1))
                        mm(mb[:, :], wq_sb[:, :], xT[fe.buf][:, :], start=True, stop=True).then_inc(q_full, 1)
                    if slot == 6 and fe.real:
                        pe.wait_ge(q_r1, fe.count(1, 1))
                        mm(mb[:, :], wk_sb[:, :], xT[fe.buf][:, :], start=True, stop=True).then_inc(k_full, 1)
                    if slot == 2 and ff.real:
                        if i.real:
                            pe.wait_ge(mT_out, i.count(2, 2))
                        else:
                            pe.wait_ge(k_r1, ff.count(1, 1))
                        for t in range(T):
                            last = mm(mb[:, 128 * t:128 * t + 128], xT[ff.buf][:, 128 * t:128 * t + 128],
                                      wv_sb[:, :], start=True, stop=True)
                        last.then_inc(v_full, 1)
                    if slot in (7, 9, 11) and ff.real:
                        c = (slot - 7) // 2
                        if c > 0:
                            pe.wait_ge(h_done, ff.count(HC, c))
                        elif fe.real:
                            pe.wait_ge(k_r1, fe.count(1, 1))
                        else:
                            pe.wait_ge(v_out, ff.count(1, 1))
                        mm(mb[:, :], wgT[:, c, :], xT[ff.buf][:, :], start=True, stop=True).then_inc(gate_full, 1)
                    if slot in (8, 10, 12) and ff.real:
                        c = (slot - 8) // 2
                        pe.wait_ge(gs_done, ff.count(HC, c + 1))
                        mm(mb[:, :], wuT[:, c, :], xT[ff.buf][:, :], start=True, stop=True).then_inc(up_full, 1)
                    if slot == 15 and ff.real:
                        pe.wait_ge(g_done, ff.count(1, 1))
                        max_T(ff, 0)
                    if slot == 13 and tail.real:
                        if ff.real:
                            pe.wait_ge(h_done, ff.count(HC, HC))
                        elif i.real:
                            pe.wait_ge(mT_out, i.count(2, 2))
                        else:
                            pe.wait_ge(y_done, tail.count(1, 0))
                        pe.wait_ge(on_ready, tail.count(1, 1))
                        for t in range(T):
                            last = mm(mb[:, 128 * t:128 * t + 128], o_norm[:, 128 * t:128 * t + 128], wo_sb[:, :],
                                      start=True, stop=True)
                        last.then_inc(out_full, 1)
                    if slot == 14 and ff.real:
                        if tail.real:
                            pe.wait_ge(y_done, tail.count(1, 1))
                        pe.wait_ge(h_done, ff.count(HC, HC))
                        for t in range(T):
                            for c in range(HC):
                                last = mm(mb[:, 128 * t:128 * t + 128], hT[:, c, 128 * t:128 * t + 128], wdT[:, c, :],
                                          start=c == 0, stop=c == HC - 1)
                        last.then_inc(down_full, 1)

            program(pe, step)


_INS = ["L0_attn_x", "L0_attn_Wq", "L0_attn_Wk", "L0_attn_Wv", "L0_attn_Wout",
        "L0_ffn_w_gate", "L0_ffn_w_up", "L0_ffn_w_down"]


def kernel(**inputs):
    import concourse.bacc as _bacc
    import numpy as _np
    from concourse import mybir as _mybir
    from concourse.bass_utils import run_bass_kernel_spmd as _run

    nc = _bacc.Bacc("TRN2", target_bir_lowering=False, num_devices=1)
    arrays, args = {}, []
    for name in _INS:
        a = _np.ascontiguousarray(inputs[name])
        arrays[f"in_{name}"] = a
        args.append(nc.dram_tensor(f"in_{name}", a.shape, _mybir.dt.from_np(a.dtype), kind="ExternalInput").ap())
    args.append(nc.dram_tensor("y", (B, L, D), _mybir.dt.float32, kind="ExternalOutput").ap())
    build(nc, *args)
    r = _run(nc, [arrays], core_ids=[0])
    return r.results[0]["y"]
```

```python
from contextlib import ExitStack

import concourse.bass as bass
from concourse import mybir

F32 = mybir.dt.float32
BF16 = mybir.dt.bfloat16
I32 = mybir.dt.int32
ACT = mybir.ActivationFunctionType
ALU = mybir.AluOpType
AX = mybir.AxisListType

B, L, D, H = 16, 512, 128, 16
E = D // H
HID = 384
T = L // 128
HC = HID // 128
TERMS = 6
Q_PART = [0, 0, 0, 1, 1, 2]
K_PART = [0, 1, 2, 0, 1, 0]
KQ = TERMS * E
KM = KQ + 2
SL = H // 2
NBUF = 3
RING = 3
U1, U2 = 44, 40
SLOTS = 20
NEWTON = 14
MASKED = -3.0e38
SCALE = 1.0 / 127.0
EPS = 1e-5
LOOP0, LOOP1 = 2, 14


class Batch:

    def __init__(self, k, off):
        self.k, self.off, self.buf = k, off, off % NBUF
        self.looped = not isinstance(k, int)
        self.first = not self.looped and off == -2

    def at(self, d):
        return Batch(self.k, self.off + d)

    @property
    def n(self):
        return self.k * NBUF + self.off if self.looped else self.off

    @property
    def real(self):
        return self.looped or 0 <= self.off < B

    def after(self, n):
        return self.looped or self.off >= n

    def count(self, per_batch, j):
        if self.looped:
            assert self.off * per_batch + j > 0
            return self.k * (NBUF * per_batch) + (self.off * per_batch + j)
        return self.off * per_batch + j

    def turns(self, j):
        if self.looped:
            assert self.off // NBUF + j > 0
            return self.k * 16 + 16 * (self.off // NBUF + j)
        return 16 * (self.off // NBUF + j)


def alone(eng, consts, value):
    if not isinstance(value, int):
        eng.lower_val(value)
        eng.wait_ge(consts, 1)
    return value


def first_pass_units(half):
    s0 = 4 * half
    pairs = [(3, [s0 + x]) for x in range(4)] + [(2, [s0 + x]) for x in range(4)]
    pairs += [(1, [s0, s0 + 1]), (1, [s0 + 2, s0 + 3]), (0, [s0 + x for x in range(4)])]
    return pairs


P1_SLOT = []
for _s in range(SLOTS):
    _h, _x = divmod(_s, 10)
    _p = _x if _x <= 4 else _x + 1
    P1_SLOT.append([11 * _h + _p] + ([11 * _h + 5] if _x == 4 else []))
P1_PAIRS = first_pass_units(0) + first_pass_units(1)

PV_SLOT = {6: (0, 0), 7: (0, 1), 8: (0, 2), 9: (0, 3), 10: (1, 0), 11: (1, 1), 12: (1, 2), 13: (1, 3),
           15: (2, 0), 16: (2, 1), 17: (2, 2), 18: (2, 3), 0: (3, 0), 1: (3, 1), 2: (3, 2), 3: (3, 3)}


def build(nc, x, wq, wk, wv, wout, wg, wu, wd, out):
    ctx = ExitStack()
    with ctx:
        def sb(name, shape, dt):
            return ctx.enter_context(nc.sbuf_tensor(name, shape, dt))

        def pb(name, shape):
            return ctx.enter_context(nc.psum_tensor(name, shape, F32))

        def sem(name):
            return ctx.enter_context(nc.semaphore(name))

        wq_nat, wk_nat = sb("wq_nat", [128, D], F32), sb("wk_nat", [128, D], F32)
        wq_sb, wk_sb = sb("wq_sb", [128, D], F32), sb("wk_sb", [128, D], F32)
        wv_sb = sb("wv_sb", [128, D], F32)
        wo_nat, wo_sb = sb("wo_nat", [128, D], F32), sb("wo_sb", [128, D], F32)
        wg_int, wu_int = sb("wg_int", [128, HC, D], I32), sb("wu_int", [128, HC, D], I32)
        wd_int = sb("wd_int", [128, HID], I32)
        wg_f, wu_f = sb("wg_f", [128, HC, D], F32), sb("wu_f", [128, HC, D], F32)
        wd_f = sb("wd_f", [128, HID], F32)
        wgT, wuT, wdT = (sb(n, [128, HC, 128], F32) for n in ("wgT", "wuT", "wdT"))
        ident = sb("ident", [128, 128], F32)
        ident_b = sb("ident_b", [128, 128], BF16)
        ones = sb("ones", [64, 128], BF16)
        causal = sb("causal", [128, L], F32)
        x_nat = [sb(f"x_nat{n}", [128, T, D], F32) for n in range(NBUF)]
        x_res = [sb(f"x_res{n}", [128, T, D], F32) for n in range(NBUF)]
        stats = sb("stats", [128, T, 6], F32)
        moments = sb("moments", [128, T, 2], F32)
        var_e, rstd, newt = sb("var_e", [128, T], F32), sb("rstd", [128, T], F32), sb("newt", [128, T], F32)
        x_hat = sb("x_hat", [128, T, D], F32)
        xT = [sb(f"xT{n}", [128, L], F32) for n in range(NBUF)]
        q_parts, k_parts = sb("q_parts", [128, 3, L], BF16), sb("k_parts", [128, 3, L], BF16)
        q_rest, k_rest = sb("q_rest", [128, L], F32), sb("k_rest", [128, L], F32)
        q_stack = [sb(f"q_stack{n}", [128, SL, L], BF16) for n in range(NBUF)]
        k_stack = [sb(f"k_stack{n}", [128, SL, L], BF16) for n in range(NBUF)]
        v_cols = [sb(f"v_cols{n}", [128, T, 2, 2, 4, 32], F32) for n in range(NBUF)]
        rowmax = sb("rowmax", [128, 2, T, 2, 4], F32)
        negmax_p = sb("negmax_p", [128, 2, T, 2, 8], BF16)
        mT_sb = sb("mT_sb", [16, 2, L], BF16)
        probs = [sb(f"probs{n}", [128, 10, L], F32) for n in range(2)]
        o_ev = sb("o_ev", [128, 2, L], F32)
        o_sb, den_sb, rden, o_norm = (sb(n, [128, L], F32) for n in ("o_sb", "den_sb", "rden", "o_norm"))
        tanh_g, gate_s = sb("tanh_g", [128, L], F32), sb("gate_s", [128, L], F32)
        hT = sb("hT", [128, HC, L], F32)
        tanh_f = sb("tanh_f", [128, L], F32)
        g_out = [sb(f"g_out{n}", [128, L], F32) for n in range(NBUF)]
        sg = sb("sg", [128, L], F32)
        y_sb = [sb(f"y_sb{n}", [128, L], F32) for n in range(NBUF)]
        s1 = [pb(f"s1_{n}", [128, 512]) for n in range(RING)]
        s2 = [pb(f"s2_{n}", [128, 512]) for n in range(RING)]
        ov = pb("ov", [128, 512])
        mb = pb("mb", [128, 512])

        w_qk, w_ffn, w_vo = sem("w_qk"), sem("w_ffn"), sem("w_vo")
        w_conv = sem("w_conv")
        w_float = sem("w_float")
        w_tr, w_ready = sem("w_tr"), sem("w_ready")
        consts = sem("consts")
        ones_in, v_set = sem("ones_in"), sem("v_set")
        x_in = [sem(f"x_in{n}") for n in range(NBUF)]
        xr_in = [sem(f"xr_in{n}") for n in range(NBUF)]
        ln_stats = sem("ln_stats")
        newton = sem("newton")
        xhat_ready = sem("xhat_ready")
        xT_full, xT_out = sem("xT_full"), sem("xT_out")
        q_full, q_hi, q_r1, q_mid, q_lo = (sem(n) for n in ("q_full", "q_hi", "q_r1", "q_mid", "q_lo"))
        k_full, k_hi, k_r1, k_mid, k_lo = (sem(n) for n in ("k_full", "k_hi", "k_r1", "k_mid", "k_lo"))
        stack_in = sem("stack_in")
        v_full, v_out = sem("v_full"), sem("v_out")
        gate_full, tanh_done, gs_done = sem("gate_full"), sem("tanh_done"), sem("gs_done")
        up_full, h_done = sem("up_full"), sem("h_done")
        down_full, tf_done, g_done = sem("down_full"), sem("tf_done"), sem("g_done")
        s1_full, s1_red = sem("s1_full"), sem("s1_red")
        nm_ready, mT_full, mT_out = sem("nm_ready"), sem("mT_full"), sem("mT_out")
        m_in = [sem(f"m_in{n}") for n in range(2)]
        s2_full, exp_done, masked = sem("s2_full"), sem("exp_done"), sem("masked")
        pv_done, ov_out = sem("pv_done"), sem("ov_out")
        o_in = [sem(f"o_in{n}") for n in range(2)]
        rden_done, on_ready = sem("rden_done"), sem("on_ready")
        out_full, y_done, fin_done = sem("out_full"), sem("y_done"), sem("fin_done")
        stored = sem("stored")
        STACK = 16 * 4 * TERMS

        def program(eng, step):
            for i in range(-2, LOOP0):
                step(Batch(0, i))
            with eng.Fori(0, (LOOP1 - LOOP0) // NBUF) as k:
                for r in range(NBUF):
                    step(Batch(k, LOOP0 + r))
            for i in range(LOOP1, B + 1):
                step(Batch(0, i))

        def tokens(t, b):
            return t[b.n].rearrange("(t p) d -> p t d", p=128)

        block = ctx.enter_context(nc.Block())

        @block.sync
        def _(sp):
            sp.dma_start(x_nat[0][:, :, :], x[0].rearrange("(t p) d -> p t d", p=128)).then_inc(x_in[0], 16)
            sp.dma_start(wq_nat[:, :], wq.rearrange("d h e -> d (h e)")).then_inc(w_qk, 16)
            sp.dma_start(wk_nat[:, :], wk.rearrange("d h e -> d (h e)")).then_inc(w_qk, 16)
            sp.dma_start(wg_int[:, :, :], wg.rearrange("(c p) d -> p c d", p=128)).then_inc(w_ffn, 16)
            sp.dma_start(wu_int[:, :, :], wu.rearrange("(c p) d -> p c d", p=128)).then_inc(w_ffn, 16)
            sp.dma_start(wd_int[:, :], wd[:, :]).then_inc(w_ffn, 16)
            sp.dma_start(wv_sb[:, :], wv.rearrange("d h e -> d (h e)")).then_inc(w_vo, 16)
            sp.dma_start(x_nat[1][:, :, :], x[1].rearrange("(t p) d -> p t d", p=128)).then_inc(x_in[1], 16)
            sp.dma_start(wo_nat[:, :], wout.rearrange("h e d -> (h e) d")).then_inc(w_vo, 16)

            def spread(parts, stack, part_of, part, b):
                for side in range(2):
                    for term in range(TERMS):
                        if part_of[term] != part:
                            continue
                        row = 64 * side + E * term
                        sp.dma_start(stack[b.buf][row:row + E, :, :],
                                     parts[64 * side:64 * side + 64, part, :]).then_inc(stack_in, 16)

            def send_max(b, half):
                sp.wait_ge(mT_out, alone(sp, consts, b.count(2, half + 1)))
                pitch = SL * L
                for part in range(2):
                    dst = bass.AP(q_stack[b.buf], (KQ + part) * pitch + 4 * half * L,
                                  [[64 * pitch, 2], [L, 4], [1, L]])
                    sp.dma_start(dst, mT_sb[8 * part:8 * part + 8, half, :]).then_inc(m_in[half], 16)

            def send_o(b, half):
                sp.wait_ge(ov_out, alone(sp, consts, b.count(2, half + 1)))
                if b.after(1):
                    sp.wait_ge(on_ready, alone(sp, consts, b.count(1, 0)))
                for dst, row in ((o_sb, 0), (den_sb, 1)):
                    sp.dma_start(dst[64 * half:64 * half + 64, :], o_ev[row::2, half, :]).then_inc(o_in[half], 16)

            def step(i):
                fe, ff, tail = i.at(2), i.at(1), i.at(-1)
                if fe.real and fe.after(2):
                    if fe.after(3):
                        sp.wait_ge(xhat_ready, alone(sp, consts, fe.at(-2).count(1, 0)))
                    sp.dma_start(x_nat[fe.buf][:, :, :], tokens(x, fe)).then_inc(x_in[fe.buf], 16)
                if i.real:
                    send_max(i, 1)
                if i.real:
                    sp.dma_start(x_res[i.buf][:, :, :], tokens(x, i)).then_inc(xr_in[i.buf], 16)
                if tail.real:
                    send_o(tail, 1)
                if fe.real:
                    if fe.after(3):
                        sp.wait_ge(s2_full, alone(sp, consts, fe.at(-2).count(U2, 0)))
                    sp.wait_ge(q_hi, alone(sp, consts, fe.count(1, 1)))
                    spread(q_parts, q_stack, Q_PART, 0, fe)
                    sp.wait_ge(k_hi, alone(sp, consts, fe.count(1, 1)))
                    spread(k_parts, k_stack, K_PART, 0, fe)
                    sp.wait_ge(q_mid, alone(sp, consts, fe.count(1, 1)))
                    spread(q_parts, q_stack, Q_PART, 1, fe)
                    sp.wait_ge(k_mid, alone(sp, consts, fe.count(1, 1)))
                    spread(k_parts, k_stack, K_PART, 1, fe)
                    sp.wait_ge(q_lo, alone(sp, consts, fe.count(1, 1)))
                    spread(q_parts, q_stack, Q_PART, 2, fe)
                    sp.wait_ge(k_lo, alone(sp, consts, fe.count(1, 1)))
                    spread(k_parts, k_stack, K_PART, 2, fe)
                if ff.real:
                    send_max(ff, 0)
                if i.real:
                    send_o(i, 0)
                if tail.real:
                    sp.wait_ge(fin_done, alone(sp, consts, tail.count(1, 1)))
                    sp.dma_start(tokens(out, tail),
                                 y_sb[tail.buf][:, :].rearrange("p (t d) -> p t d", t=T)).then_inc(stored, 16)

            program(sp, step)
            sp.wait_ge(stored, 16 * B)

        @block.gpsimd
        def _(pool):
            nc.gpsimd.memset(ident[:, :], 1.0)
            nc.gpsimd.memset(causal[:, :], 0.0).then_inc(w_conv, 1)
            pool.wait_ge(w_conv, 1)
            nc.gpsimd.affine_select(out=ident[:, :], in_=ident[:, :], compare_op=ALU.is_equal, fill=0.0,
                                    base=0, pattern=[[1, 128]], channel_multiplier=-1).then_inc(w_conv, 1)
            diag = causal[:, L - 128:]
            nc.gpsimd.affine_select(out=diag, in_=diag, compare_op=ALU.is_ge, fill=MASKED,
                                    base=0, pattern=[[-1, 128]], channel_multiplier=1).then_inc(w_conv, 1)

            def rsqrt(b):
                pool.wait_ge(ln_stats, alone(pool, consts, b.count(2, 2)))
                if b.after(1):
                    pool.wait_ge(xhat_ready, alone(pool, consts, b.count(1, 0)))
                nc.gpsimd.tensor_scalar(var_e[:, :], moments[:, :, 1], EPS, None, ALU.add).then_inc(newton, 1)
                pool.wait_ge(newton, alone(pool, consts, b.count(NEWTON, 1)))
                nc.gpsimd.tensor_scalar(rstd[:, :].bitcast(I32), var_e[:, :].bitcast(I32),
                                        -0.5, float(0x5F3759DF), ALU.mult, ALU.add).then_inc(newton, 1)
                for n in range(3):
                    pool.wait_ge(newton, alone(pool, consts, b.count(NEWTON, 4 * n + 2)))
                    nc.gpsimd.tensor_tensor(newt[:, :], rstd[:, :], rstd[:, :], ALU.mult).then_inc(newton, 1)
                    pool.wait_ge(newton, alone(pool, consts, b.count(NEWTON, 4 * n + 3)))
                    nc.gpsimd.tensor_tensor(newt[:, :], newt[:, :], var_e[:, :], ALU.mult).then_inc(newton, 1)
                    pool.wait_ge(newton, alone(pool, consts, b.count(NEWTON, 4 * n + 4)))
                    nc.gpsimd.tensor_scalar(newt[:, :], newt[:, :], -0.5, 1.5,
                                            ALU.mult, ALU.add).then_inc(newton, 1)
                    pool.wait_ge(newton, alone(pool, consts, b.count(NEWTON, 4 * n + 5)))
                    nc.gpsimd.tensor_tensor(rstd[:, :], rstd[:, :], newt[:, :], ALU.mult).then_inc(newton, 1)

            def mask(b, slot):
                g, r = divmod(slot, 5)
                pool.wait_ge(exp_done, alone(pool, consts, b.count(U2, 2 * slot + 2)))
                pair = probs[g % 2][:, 2 * r:2 * r + 2, :].rearrange("p u (n c) -> p u n c", c=128)
                if r < 2:
                    parts = [pair[:, :, 0, :]]
                elif r < 4:
                    parts = [pair[:, 0, 0::3, :], pair[:, 1, 0::3, :]]
                else:
                    parts = [pair[:, :, :, :].rearrange("p u n c -> p (u n) c")[:, 0::2, :]]
                for part in parts:
                    nc.gpsimd.affine_select(out=part, in_=part, compare_op=ALU.is_ge, fill=0.0, base=0,
                                            pattern=[[0, part.shape[1]], [1, 128]],
                                            channel_multiplier=-1).then_inc(masked, 1)

            def step(i):
                fe, tail = i.at(2), i.at(-1)
                for slot in range(SLOTS):
                    if i.real:
                        mask(i, slot)
                    if slot == 0 and fe.real:
                        rsqrt(fe)
                    if slot == 8 and fe.real:
                        pool.wait_ge(q_mid, alone(pool, consts, fe.count(1, 1)))
                        nc.gpsimd.tensor_tensor(q_parts[:, 2, :], q_rest[:, :], q_parts[:, 1, :],
                                                ALU.subtract).then_inc(q_lo, 1)
                    if slot == 9 and fe.real:
                        pool.wait_ge(k_mid, alone(pool, consts, fe.count(1, 1)))
                        nc.gpsimd.tensor_tensor(k_parts[:, 2, :], k_rest[:, :], k_parts[:, 1, :],
                                                ALU.subtract).then_inc(k_lo, 1)
                    if slot == 10 and tail.real:
                        pool.wait_ge(rden_done, alone(pool, consts, tail.count(4, 4)))
                        if tail.after(1):
                            pool.wait_ge(out_full, alone(pool, consts, tail.count(1, 0)))
                        nc.gpsimd.tensor_tensor(o_norm[:, :], o_sb[:, :], rden[:, :], ALU.mult).then_inc(on_ready, 1)
                    if slot == 15 and tail.real:
                        if tail.after(1):
                            pool.wait_ge(stored, alone(pool, consts, tail.count(16, 0)))
                        pool.wait_ge(xr_in[tail.buf], alone(pool, consts, tail.turns(1)))
                        pool.wait_ge(y_done, alone(pool, consts, tail.count(1, 1)))
                        nc.gpsimd.tensor_tensor(y_sb[tail.buf][:, :], sg[:, :],
                                                x_res[tail.buf][:, :, :].rearrange("p t d -> p (t d)"),
                                                ALU.add).then_inc(fin_done, 1)

            program(pool, step)

        @block.scalar
        def _(act):
            def copy(dst, src):
                return nc.scalar.activation(dst, src, ACT.Copy)

            def ffn_weights_out():
                for n, (dst, src) in enumerate(((wgT, ov), (wuT, s2[0]), (wdT, s2[1]))):
                    act.wait_ge(w_tr, n + 1)
                    copy(dst[:, :, :].rearrange("p c m -> p (c m)"), src[:, 0:HID]).then_inc(w_ready, 1)

            def ones_rows():
                act.wait_ge(consts, 1)
                pitch = SL * L
                for n in range(NBUF):
                    for part in range(2):
                        dst = bass.AP(k_stack[n], (KQ + part) * pitch, [[64 * pitch, 2], [128, SL * L // 128], [1, 128]])
                        act.dma_start(dst, ones[:, :]).then_inc(ones_in, 16)

            def exp_unit(b, slot, side):
                g, r = divmod(slot, 5)
                u = 2 * slot + side
                if r == 0 and side == 0:
                    if b.after(1) or g > 1:
                        act.wait_ge(pv_done, b.count(16, 4 * (g - 1)))
                act.wait_ge(s2_full, b.count(U2, u + 1))
                nc.scalar.activation(probs[g % 2][:, 2 * r + side, :], s2[(U2 * b.off + u) % RING][:, :],
                                     ACT.Exp, scale=float(E) ** -0.5).then_inc(exp_done, 1)

            def step(i):
                fe, ff, tail = i.at(2), i.at(1), i.at(-1)
                for slot in range(SLOTS):
                    if slot == 2 and i.real:
                        max_out(i, 1)
                    if slot == 16 and ff.real:
                        max_out(ff, 0)
                    if slot == 10 and i.first:
                        ffn_weights_out()
                        ones_rows()
                    if slot == 3 and ff.real:
                        if ff.after(3):
                            act.wait_ge(pv_done, ff.at(-2).count(16, 0))
                        if i.off < LOOP0 and not i.looped:
                            act.wait_ge(v_set, 2)
                        act.wait_ge(v_full, ff.count(1, 1))
                        dst = v_cols[ff.buf][:, :, :, :, :, :].rearrange("p t f s c m -> p (t f) s c m")
                        src = mb[:, :].rearrange("p (g c s e) -> p g s c e", c=4, s=2, e=E)
                        copy(dst[:, :, 0, :, 0:2 * E:2], src[:, :, 0])
                        copy(dst[:, :, 1, :, 2 * E:4 * E:2], src[:, :, 1]).then_inc(v_out, 1)
                    if slot == 5 and fe.real:
                        if fe.after(3):
                            act.wait_ge(up_full, fe.at(-2).count(HC, 0))
                        act.wait_ge(xT_full, fe.count(1, 1))
                        copy(xT[fe.buf][:, :], mb[:, :]).then_inc(xT_out, 1)
                    if slot == 6 and fe.real:
                        if fe.after(1):
                            act.wait_ge(stack_in, fe.count(STACK, 0))
                        act.wait_ge(q_full, fe.count(1, 1))
                        copy(q_parts[:, 0, :], mb[:, :]).then_inc(q_hi, 1)
                    if slot == 7 and fe.real:
                        act.wait_ge(k_full, fe.count(1, 1))
                        copy(k_parts[:, 0, :], mb[:, :]).then_inc(k_hi, 1)
                        act.wait_ge(q_r1, fe.count(1, 1))
                        copy(q_parts[:, 1, :], q_rest[:, :]).then_inc(q_mid, 1)
                    if slot == 8 and fe.real:
                        act.wait_ge(k_r1, fe.count(1, 1))
                        copy(k_parts[:, 1, :], k_rest[:, :]).then_inc(k_mid, 1)
                    if slot in (8, 10, 12) and ff.real:
                        c = (slot - 8) // 2
                        if ff.after(1) or c > 0:
                            act.wait_ge(gs_done, ff.count(HC, c))
                        act.wait_ge(gate_full, ff.count(HC, c + 1))
                        nc.scalar.activation(tanh_g[:, :], mb[:, :], ACT.Tanh, scale=0.5).then_inc(tanh_done, 1)
                    if slot == 15 and ff.real:
                        if ff.after(1):
                            act.wait_ge(g_done, ff.count(1, 0))
                        act.wait_ge(down_full, ff.count(1, 1))
                        nc.scalar.activation(tanh_f[:, :], mb[:, :], ACT.Tanh, scale=0.5).then_inc(tf_done, 1)
                    if slot == 4 and tail.real:
                        heads_out(tail, 1)
                    if slot == 14 and i.real:
                        heads_out(i, 0)
                    if i.real:
                        exp_unit(i, slot, 0)
                        exp_unit(i, slot, 1)

            def max_out(b, half):
                if b.after(1):
                    act.wait_ge(m_in[half], b.count(32, 0))
                act.wait_ge(mT_full, b.count(2, half + 1))
                copy(mT_sb[:, half, :], mb[0:16, :]).then_inc(mT_out, 1)

            def heads_out(b, half):
                if b.after(1):
                    act.wait_ge(o_in[half], b.count(32, 0))
                act.wait_ge(pv_done, b.count(16, 8 * half + 8))
                copy(o_ev[:, half, :], ov[:, :]).then_inc(ov_out, 1)

            program(act, step)

        @block.vector
        def _(dve):
            nc.vector.memset(ones[:, :], 1.0).then_inc(consts, 1)
            dve.wait_ge(w_conv, 2)
            nc.vector.tensor_copy(ident_b[:, :], ident[:, :]).then_inc(consts, 1)

            def qk_weights():
                dve.wait_ge(w_qk, 32)
                for nat, dst in ((wq_nat, wq_sb), (wk_nat, wk_sb)):
                    src = nat[:, :].rearrange("p (f d a s e) -> p f a e s d", f=2, d=2, a=2, s=2)
                    to = dst[:, :].rearrange("p (a e f s d) -> p f a e s d", a=2, e=E, f=2, s=2)
                    for f in range(2):
                        for a in range(2):
                            last = nc.vector.tensor_copy(to[:, f, a], src[:, f, a])
                last.then_inc(w_float, 1)

            def other_weights():
                dve.wait_ge(w_ffn, 48)
                nc.vector.tensor_scalar(wg_f[:, :, :], wg_int[:, :, :], SCALE, None, ALU.mult)
                nc.vector.tensor_scalar(wu_f[:, :, :], wu_int[:, :, :], SCALE, None, ALU.mult)
                nc.vector.tensor_scalar(wd_f[:, :], wd_int[:, :], SCALE, 0.5, ALU.mult, ALU.mult)
                dve.wait_ge(w_vo, 32)
                nc.vector.tensor_scalar(wo_sb[:, :], wo_nat[:, :], 0.5, None, ALU.mult).then_inc(w_float, 1)

            def v_constants():
                for n in range(NBUF):
                    last = nc.vector.memset(v_cols[n][:, :, :, :, :, :].rearrange("p t f s c m -> p (t f s c m)"), 0.0)
                last.then_inc(v_set, 1)
                dve.wait_ge(v_set, 1)
                for n in range(NBUF):
                    cols = v_cols[n][:, :, :, :, :, :].rearrange("p t f s c m -> p (t f) s c m")
                    nc.vector.memset(cols[:, :, 0, :, 1:2 * E:2], 1.0)
                    last = nc.vector.memset(cols[:, :, 1, :, 2 * E + 1:4 * E:2], 1.0)
                last.then_inc(v_set, 1)

            def reduce_units(b, pair):
                tile, slots = P1_PAIRS[pair]
                half, width = pair // 11, 128 * (tile + 1)
                for side in range(2):
                    u = 2 * pair + side
                    dve.wait_ge(s1_full, alone(dve, consts, b.count(U1, u + 1)))
                    bank = s1[(U1 * b.off + u) % RING]
                    for n, s in enumerate(slots):
                        at = s - 4 * half
                        scores = bank[:, n * width:(n + 1) * width]
                        last = nc.vector.tensor_tensor_reduce(scores, scores, causal[:, L - width:], 1.0, MASKED,
                                                              ALU.add, ALU.max, rowmax[:, half, tile, side, at:at + 1])
                    last.then_inc(s1_red, 1)

            def split_max(b, half):
                if b.after(1):
                    dve.wait_ge(mT_full, b.at(-1).count(2, half + 1))
                dve.wait_ge(s1_red, b.count(U1, 22 * (half + 1)))
                src = rowmax[:, half].rearrange("p t a s -> p t (a s)")
                nc.vector.tensor_scalar(negmax_p[:, half, :, 0, :], src, -1.0, None, ALU.mult).then_inc(nm_ready, 1)
                dve.wait_ge(nm_ready, b.count(4, 2 * half + 1))
                nc.vector.scalar_tensor_tensor(negmax_p[:, half, :, 1, :], src, -1.0, negmax_p[:, half, :, 0, :],
                                               ALU.mult, ALU.subtract).then_inc(nm_ready, 1)

            def step(i):
                fe, ff, tail = i.at(2), i.at(1), i.at(-1)
                for slot in range(SLOTS):
                    if slot == 0 and fe.real:
                        dve.wait_ge(x_in[fe.buf], fe.turns(1))
                        for t in range(T):
                            last = nc.vector.bn_stats(stats[:, t, :], x_nat[fe.buf][:, t, :])
                        last.then_inc(ln_stats, 1)
                        if fe.after(1):
                            dve.wait_ge(newton, fe.count(NEWTON, 0))
                        dve.wait_ge(ln_stats, alone(dve, consts, fe.count(2, 1)))
                        for t in range(T):
                            last = nc.vector.bn_aggr(moments[:, t, :], stats[:, t, :])
                        last.then_inc(ln_stats, 1)
                    if slot == 1 and i.first:
                        qk_weights()
                    if slot == 10 and i.first:
                        other_weights()
                        v_constants()
                    if slot == 3 and fe.real:
                        if fe.after(1):
                            dve.wait_ge(xT_full, fe.count(1, 0))
                        dve.wait_ge(newton, fe.count(NEWTON, NEWTON))
                        for t in range(T):
                            last = nc.vector.tensor_scalar(x_hat[:, t, :], x_nat[fe.buf][:, t, :],
                                                           moments[:, t, 0:1], rstd[:, t:t + 1],
                                                           ALU.subtract, ALU.mult)
                        last.then_inc(xhat_ready, 1)
                    if slot == 6 and fe.real:
                        if fe.after(1):
                            dve.wait_ge(q_lo, fe.count(1, 0))
                        dve.wait_ge(q_hi, fe.count(1, 1))
                        nc.vector.tensor_tensor(q_rest[:, :], mb[:, :], q_parts[:, 0, :], ALU.subtract).then_inc(q_r1, 1)
                    if slot == 7 and fe.real:
                        if fe.after(1):
                            dve.wait_ge(k_lo, fe.count(1, 0))
                        dve.wait_ge(k_hi, fe.count(1, 1))
                        nc.vector.tensor_tensor(k_rest[:, :], mb[:, :], k_parts[:, 0, :], ALU.subtract).then_inc(k_r1, 1)
                    if slot in (8, 10, 12) and ff.real:
                        c = (slot - 8) // 2
                        if ff.after(1) or c > 0:
                            dve.wait_ge(h_done, ff.count(HC, c))
                        dve.wait_ge(tanh_done, ff.count(HC, c + 1))
                        nc.vector.scalar_tensor_tensor(gate_s[:, :], tanh_g[:, :], 1.0, mb[:, :],
                                                       ALU.add, ALU.mult).then_inc(gs_done, 1)
                    if slot in (9, 11, 13) and ff.real:
                        c = (slot - 9) // 2
                        if ff.after(1):
                            dve.wait_ge(down_full, ff.count(1, 0))
                        dve.wait_ge(gs_done, ff.count(HC, c + 1))
                        dve.wait_ge(up_full, ff.count(HC, c + 1))
                        nc.vector.tensor_tensor(hT[:, c, :], gate_s[:, :], mb[:, :], ALU.mult).then_inc(h_done, 1)
                    if slot in (6, 7, 8, 9) and tail.real:
                        n = slot - 6
                        if n == 0:
                            if tail.after(1):
                                dve.wait_ge(on_ready, tail.count(1, 0))
                            dve.wait_ge(o_in[0], tail.count(32, 32))
                            dve.wait_ge(o_in[1], tail.count(32, 32))
                        nc.vector.reciprocal(rden[:, 128 * n:128 * n + 128],
                                             den_sb[:, 128 * n:128 * n + 128]).then_inc(rden_done, 1)
                    if slot == 14 and tail.real:
                        if tail.after(1):
                            dve.wait_ge(fin_done, tail.count(1, 0))
                        dve.wait_ge(g_done, tail.count(1, 1))
                        dve.wait_ge(out_full, tail.count(1, 1))
                        nc.vector.tensor_tensor(sg[:, :], g_out[tail.buf][:, :], mb[:, :], ALU.mult).then_inc(y_done, 1)
                    if slot == 15 and ff.real:
                        dve.wait_ge(tf_done, ff.count(1, 1))
                        if ff.after(3):
                            dve.wait_ge(y_done, ff.at(-2).count(1, 0))
                        nc.vector.scalar_tensor_tensor(g_out[ff.buf][:, :], tanh_f[:, :], 1.0, mb[:, :],
                                                       ALU.add, ALU.mult).then_inc(g_done, 1)
                    if ff.real:
                        for pair in P1_SLOT[slot]:
                            reduce_units(ff, pair)
                        if slot == 9:
                            split_max(ff, 0)
                        if slot == 19:
                            split_max(ff, 1)

            program(dve, step)

        @block.tensor
        def _(pe):
            mm = nc.tensor.matmul

            def ffn_weights():
                pe.wait_ge(w_float, 2)
                for w, bank in ((wg_f, ov), (wu_f, s2[0])):
                    for c in range(HC):
                        last = nc.tensor.transpose(bank[:, 128 * c:128 * c + 128], w[:, c, :], ident[:, :])
                    last.then_inc(w_tr, 1)
                for c in range(HC):
                    last = nc.tensor.transpose(s2[1][:, 128 * c:128 * c + 128],
                                               wd_f[:, 128 * c:128 * c + 128], ident[:, :])
                last.then_inc(w_tr, 1)
                pe.wait_ge(w_ready, 3)

            def pass1(b, pair):
                tile, slots = P1_PAIRS[pair]
                width = 128 * (tile + 1)
                if pair == 0:
                    pe.wait_ge(stack_in, b.count(STACK, STACK))
                for side in range(2):
                    u = 2 * pair + side
                    if b.after(1) or u >= RING:
                        pe.wait_ge(s1_red, b.count(U1, u + 1 - RING))
                    rows = slice(64 * side, 64 * side + KQ)
                    for n, s in enumerate(slots):
                        last = mm(s1[(U1 * b.off + u) % RING][:, n * width:(n + 1) * width],
                                  q_stack[b.buf][rows, s, 128 * tile:128 * tile + 128],
                                  k_stack[b.buf][rows, s, 0:width], start=True, stop=True)
                    last.then_inc(s1_full, 1)

            def pass2(b, slot):
                g, r = divmod(slot, 5)
                if slot == 0 and not b.looped and b.off < LOOP0:
                    pe.wait_ge(ones_in, 16 * 2 * NBUF)
                if slot in (0, 10):
                    pe.wait_ge(m_in[slot // 10], b.count(32, 32))
                jobs = {0: [(2 * g, 0, 0)], 1: [(2 * g + 1, 0, 0)],
                        2: [(2 * g, 1, 0), (2 * g, 3, 384)], 3: [(2 * g + 1, 1, 0), (2 * g + 1, 3, 384)],
                        4: [(2 * g, 2, 0), (2 * g + 1, 2, 256)]}[r]
                for n, (s, j, col) in enumerate(jobs):
                    for side in range(2):
                        u = 2 * slot + side
                        if n == 0:
                            if b.after(1) or u >= RING:
                                pe.wait_ge(exp_done, b.count(U2, u + 1 - RING))
                        rows = slice(64 * side, 64 * side + KM)
                        last = mm(s2[(U2 * b.off + u) % RING][:, col:col + L - 128 * j],
                                  k_stack[b.buf][rows, s, 128 * j:128 * j + 128],
                                  q_stack[b.buf][rows, s, 128 * j:L], start=True, stop=True)
                        if n == len(jobs) - 1:
                            last.then_inc(s2_full, 1)

            def attend(b, g, j):
                half, sub = divmod(g, 2)
                if g == 0 and j == 0:
                    pe.wait_ge(v_out, b.count(1, 1))
                if sub == 0 and j == 0:
                    if b.after(1) or half > 0:
                        pe.wait_ge(ov_out, b.count(2, half))
                pe.wait_ge(masked, b.count(28, 7 * g + (2, 6, 7, 7)[j]))
                for c in range(4):
                    side, d = c % 2, c // 2
                    unit, col = {0: (d, 0), 1: (2 + d, 0), 2: (4, 256 * d), 3: (2 + d, 384)}[j]
                    last = mm(ov[32 * c:32 * c + 32, 128 * j:L], v_cols[b.buf][:, j, half, sub, c, :],
                              probs[g % 2][:, 2 * unit + side, col:col + L - 128 * j],
                              start=sub == 0 and j == 0, stop=sub == 1 and j == 3, skip_group_check=True)
                last.then_inc(pv_done, 1)

            def max_T(b, half):
                pe.wait_ge(nm_ready, b.count(4, 2 * half + 2))
                for t in range(T):
                    last = mm(mb[0:16, 128 * t:128 * t + 128],
                              negmax_p[:, half, t].rearrange("p a h -> p (a h)"), ident_b[:, :], start=True, stop=True)
                last.then_inc(mT_full, 1)

            def step(i):
                fe, ff, tail = i.at(2), i.at(1), i.at(-1)
                for slot in range(SLOTS):
                    if ff.real:
                        for pair in P1_SLOT[slot]:
                            pass1(ff, pair)
                    if i.real:
                        pass2(i, slot)
                    if slot in PV_SLOT:
                        g, j = PV_SLOT[slot]
                        b = tail if g == 3 else i
                        if b.real:
                            attend(b, g, j)
                    if slot == 1 and i.real:
                        pe.wait_ge(mT_out, i.count(2, 1))
                        max_T(i, 1)
                    if slot == 4 and fe.real:
                        if ff.real:
                            pe.wait_ge(v_out, ff.count(1, 1))
                        pe.wait_ge(xhat_ready, fe.count(1, 1))
                        if i.first:
                            pe.wait_ge(w_conv, 2)
                        for t in range(T):
                            last = nc.tensor.transpose(mb[:, 128 * t:128 * t + 128], x_hat[:, t, :], ident[:, :])
                        last.then_inc(xT_full, 1)
                    if slot == 5 and i.first:
                        pe.wait_ge(w_float, 1)
                    if slot == 10 and i.first:
                        ffn_weights()
                        pe.wait_ge(consts, 2)
                    if slot == 5 and fe.real:
                        pe.wait_ge(xT_out, fe.count(1, 1))
                        mm(mb[:, :], wq_sb[:, :], xT[fe.buf][:, :], start=True, stop=True).then_inc(q_full, 1)
                    if slot == 6 and fe.real:
                        pe.wait_ge(q_r1, fe.count(1, 1))
                        mm(mb[:, :], wk_sb[:, :], xT[fe.buf][:, :], start=True, stop=True).then_inc(k_full, 1)
                    if slot == 2 and ff.real:
                        if i.real:
                            pe.wait_ge(mT_out, i.count(2, 2))
                        else:
                            pe.wait_ge(k_r1, ff.count(1, 1))
                        for t in range(T):
                            last = mm(mb[:, 128 * t:128 * t + 128], xT[ff.buf][:, 128 * t:128 * t + 128],
                                      wv_sb[:, :], start=True, stop=True)
                        last.then_inc(v_full, 1)
                    if slot in (7, 9, 11) and ff.real:
                        c = (slot - 7) // 2
                        if c > 0:
                            pe.wait_ge(h_done, ff.count(HC, c))
                        elif fe.real:
                            pe.wait_ge(k_r1, fe.count(1, 1))
                        else:
                            pe.wait_ge(v_out, ff.count(1, 1))
                        mm(mb[:, :], wgT[:, c, :], xT[ff.buf][:, :], start=True, stop=True).then_inc(gate_full, 1)
                    if slot in (8, 10, 12) and ff.real:
                        c = (slot - 8) // 2
                        pe.wait_ge(gs_done, ff.count(HC, c + 1))
                        mm(mb[:, :], wuT[:, c, :], xT[ff.buf][:, :], start=True, stop=True).then_inc(up_full, 1)
                    if slot == 15 and ff.real:
                        pe.wait_ge(g_done, ff.count(1, 1))
                        max_T(ff, 0)
                    if slot == 13 and tail.real:
                        if ff.real:
                            pe.wait_ge(h_done, ff.count(HC, HC))
                        elif i.real:
                            pe.wait_ge(mT_out, i.count(2, 2))
                        else:
                            pe.wait_ge(y_done, tail.count(1, 0))
                        pe.wait_ge(on_ready, tail.count(1, 1))
                        for t in range(T):
                            last = mm(mb[:, 128 * t:128 * t + 128], o_norm[:, 128 * t:128 * t + 128], wo_sb[:, :],
                                      start=True, stop=True)
                        last.then_inc(out_full, 1)
                    if slot == 14 and ff.real:
                        if tail.real:
                            pe.wait_ge(y_done, tail.count(1, 1))
                        pe.wait_ge(h_done, ff.count(HC, HC))
                        for t in range(T):
                            for c in range(HC):
                                last = mm(mb[:, 128 * t:128 * t + 128], hT[:, c, 128 * t:128 * t + 128], wdT[:, c, :],
                                          start=c == 0, stop=c == HC - 1)
                        last.then_inc(down_full, 1)

            program(pe, step)


_INS = ["L0_attn_x", "L0_attn_Wq", "L0_attn_Wk", "L0_attn_Wv", "L0_attn_Wout",
        "L0_ffn_w_gate", "L0_ffn_w_up", "L0_ffn_w_down"]


def kernel(**inputs):
    import concourse.bacc as _bacc
    import numpy as _np
    from concourse import mybir as _mybir
    from concourse.bass_utils import run_bass_kernel_spmd as _run

    nc = _bacc.Bacc("TRN2", target_bir_lowering=False, num_devices=1)
    arrays, args = {}, []
    for name in _INS:
        a = _np.ascontiguousarray(inputs[name])
        arrays[f"in_{name}"] = a
        args.append(nc.dram_tensor(f"in_{name}", a.shape, _mybir.dt.from_np(a.dtype), kind="ExternalInput").ap())
    args.append(nc.dram_tensor("y", (B, L, D), _mybir.dt.float32, kind="ExternalOutput").ap())
    build(nc, *args)
    r = _run(nc, [arrays], core_ids=[0])
    return r.results[0]["y"]
```

```python
from contextlib import ExitStack

import concourse.bass as bass
from concourse import mybir

F32 = mybir.dt.float32
BF16 = mybir.dt.bfloat16
I32 = mybir.dt.int32
ACT = mybir.ActivationFunctionType
ALU = mybir.AluOpType

B, L, D, H = 16, 512, 128, 16
E = D // H
HID = 384
T = L // 128
HC = HID // 128
TERMS = 6
Q_PART = [0, 0, 0, 1, 1, 2]
K_PART = [0, 1, 2, 0, 1, 0]
KQ = TERMS * E
KM = KQ + 2
SL = H // 2
NBUF = 3
RING1, RING2 = 3, 2
U1, U2 = 44, 40
SLOTS = 20
LEAD = 6
NEWTON = 14
MASKED = -3.0e38
SCALE = 1.0 / 127.0
EPS = 1e-5
LOOP0, LOOP1 = 2, 14


class Batch:

    def __init__(self, k, off):
        self.k, self.off, self.buf = k, off, off % NBUF
        self.looped = not isinstance(k, int)
        self.first = not self.looped and off == -2
        self.second = not self.looped and off == -1

    def at(self, d):
        return Batch(self.k, self.off + d)

    @property
    def n(self):
        return self.k * NBUF + self.off if self.looped else self.off

    @property
    def real(self):
        return self.looped or 0 <= self.off < B

    def after(self, n):
        return self.looped or self.off >= n

    def count(self, per_batch, j):
        if self.looped:
            assert self.off * per_batch + j > 0
            return self.k * (NBUF * per_batch) + (self.off * per_batch + j)
        return self.off * per_batch + j

    def turns(self, j):
        if self.looped:
            assert self.off // NBUF + j > 0
            return self.k * 16 + 16 * (self.off // NBUF + j)
        return 16 * (self.off // NBUF + j)


def slots_of(i):
    if i.second:
        return [(s if s >= 0 else None, s + LEAD if s + LEAD < SLOTS else None) for s in range(-LEAD, SLOTS)]
    return [(slot, slot) for slot in range(SLOTS)]


def alone(eng, consts, value):
    if not isinstance(value, int):
        eng.lower_val(value)
        eng.wait_ge(consts, 1)
    return value


def first_pass_units(half):
    s0 = 4 * half
    banks = [(2, [s0 + x]) for x in range(4)] + [(3, [s0 + x]) for x in range(4)]
    banks += [(1, [s0, s0 + 1]), (1, [s0 + 2, s0 + 3]), (0, [s0 + x for x in range(4)])]
    return [(tile, slots, side) for tile, slots in banks for side in range(2)]


P1_UNITS = first_pass_units(0) + first_pass_units(1)
P1_SLOT = []
for _per in (2, 2, 2, 2, 2, 2, 3, 3, 2, 2) + (2, 3, 3, 2, 2, 2, 2, 2, 2, 2):
    _n = sum(len(_units) for _units in P1_SLOT)
    P1_SLOT.append(list(range(_n, _n + _per)))

PV_SLOT = {first + j: (g, j) for g, first in ((0, 6), (1, 11), (2, 16), (3, 1)) for j in range(T)}
GATE_MADE, GATE_READ = (0, 3, 9), (1, 4, 10)
UP_MADE, UP_READ = (1, 4, 10), (2, 5, 11)
DOWN_MADE = (12, 13, 14)


def build(nc, x, wq, wk, wv, wout, wg, wu, wd, out):
    ctx = ExitStack()
    with ctx:
        def sb(name, shape, dt):
            return ctx.enter_context(nc.sbuf_tensor(name, shape, dt))

        def pb(name, shape):
            return ctx.enter_context(nc.psum_tensor(name, shape, F32))

        def sem(name):
            return ctx.enter_context(nc.semaphore(name))

        wq_nat, wk_nat = sb("wq_nat", [128, D], F32), sb("wk_nat", [128, D], F32)
        wq_sb, wk_sb = sb("wq_sb", [128, D], F32), sb("wk_sb", [128, D], F32)
        wv_sb = sb("wv_sb", [128, D], F32)
        wo_nat, wo_sb = sb("wo_nat", [128, D], F32), sb("wo_sb", [128, D], F32)
        wg_int, wu_int = sb("wg_int", [128, HC, D], I32), sb("wu_int", [128, HC, D], I32)
        wd_int = sb("wd_int", [128, HID], I32)
        wg_f, wu_f = sb("wg_f", [128, HC, D], F32), sb("wu_f", [128, HC, D], F32)
        wd_f = sb("wd_f", [128, HID], F32)
        wgT, wuT, wdT = (sb(n, [128, HC, 128], F32) for n in ("wgT", "wuT", "wdT"))
        ident = sb("ident", [128, 128], F32)
        ident_b = sb("ident_b", [128, 128], BF16)
        ones = sb("ones", [64, 128], BF16)
        causal = sb("causal", [128, L], F32)
        x_nat = [sb(f"x_nat{n}", [128, T, D], F32) for n in range(NBUF)]
        x_res = [sb(f"x_res{n}", [128, T, D], F32) for n in range(NBUF)]
        stats = sb("stats", [128, T, 6], F32)
        moments = sb("moments", [128, T, 2], F32)
        var_e, rstd, newt = sb("var_e", [128, T], F32), sb("rstd", [128, T], F32), sb("newt", [128, T], F32)
        x_hat = sb("x_hat", [128, T, D], F32)
        xT = [sb(f"xT{n}", [128, L], F32) for n in range(NBUF)]
        q_parts, k_parts = sb("q_parts", [128, 3, L], BF16), sb("k_parts", [128, 3, L], BF16)
        q_rest, k_rest = sb("q_rest", [128, L], F32), sb("k_rest", [128, L], F32)
        q_stack = [sb(f"q_stack{n}", [128, SL, L], BF16) for n in range(NBUF)]
        k_stack = [sb(f"k_stack{n}", [128, SL, L], BF16) for n in range(NBUF)]
        v_cols = [sb(f"v_cols{n}", [128, T, 2, 2, 4, 32], F32) for n in range(NBUF)]
        rowmax = sb("rowmax", [128, 2, T, 2, 4], F32)
        negmax_p = sb("negmax_p", [128, 2, T, 2, 8], BF16)
        mT_sb = sb("mT_sb", [16, 2, L], BF16)
        probs = [sb(f"probs{n}", [128, 10, L], F32) for n in range(2)]
        o_ev = sb("o_ev", [128, 2, L], F32)
        o_sb, rden, o_norm = (sb(n, [128, L], F32) for n in ("o_sb", "rden", "o_norm"))
        sums, rsums = sb("sums", [128, 128], F32), sb("rsums", [128, 128], F32)
        tanh_g, gate_s = sb("tanh_g", [128, L], F32), sb("gate_s", [128, HC, L], F32)
        hT = sb("hT", [128, HC, L], F32)
        tanh_f = sb("tanh_f", [128, L], F32)
        g_out = [sb(f"g_out{n}", [128, L], F32) for n in range(NBUF)]
        sg = sb("sg", [128, L], F32)
        y_sb = [sb(f"y_sb{n}", [128, L], F32) for n in range(NBUF)]
        s1 = [pb(f"s1_{n}", [128, 512]) for n in range(RING1)]
        s2 = [pb(f"s2_{n}", [128, 512]) for n in range(RING2)]
        ov = pb("ov", [128, 512])
        mb_a, mb_b = pb("mb_a", [128, 512]), pb("mb_b", [128, 512])

        w_qk, w_ffn, w_vo = sem("w_qk"), sem("w_ffn"), sem("w_vo")
        w_conv = sem("w_conv")
        w_float = sem("w_float")
        w_tr, w_ready = sem("w_tr"), sem("w_ready")
        consts = sem("consts")
        ones_in, v_set = sem("ones_in"), sem("v_set")
        x_in = [sem(f"x_in{n}") for n in range(NBUF)]
        xr_in = [sem(f"xr_in{n}") for n in range(NBUF)]
        ln_stats = sem("ln_stats")
        newton = sem("newton")
        xhat_ready = sem("xhat_ready")
        xT_full, xT_out = sem("xT_full"), sem("xT_out")
        q_f, k_f, up_out = sem("q_f"), sem("k_f"), sem("up_out")
        q_full, q_hi, q_r1, q_mid, q_lo = (sem(n) for n in ("q_full", "q_hi", "q_r1", "q_mid", "q_lo"))
        k_full, k_hi, k_r1, k_mid, k_lo = (sem(n) for n in ("k_full", "k_hi", "k_r1", "k_mid", "k_lo"))
        stack_in = sem("stack_in")
        v_full, v_out = sem("v_full"), sem("v_out")
        gate_full, tanh_done, gs_done = sem("gate_full"), sem("tanh_done"), sem("gs_done")
        up_full, h_done = sem("up_full"), sem("h_done")
        down_full, tf_done, g_done = sem("down_full"), sem("tf_done"), sem("g_done")
        s1_full, s1_red = sem("s1_full"), sem("s1_red")
        nm_ready, mT_full, mT_out = sem("nm_ready"), sem("mT_full"), sem("mT_out")
        m_in = [sem(f"m_in{n}") for n in range(2)]
        s2_full, exp_done, masked = sem("s2_full"), sem("exp_done"), sem("masked")
        pv_done, ov_out = sem("pv_done"), sem("ov_out")
        o_in = [sem(f"o_in{n}") for n in range(2)]
        rsum_done, rden_in, on_ready = sem("rsum_done"), sem("rden_in"), sem("on_ready")
        out_full, y_done, yT_full, fin_done = sem("out_full"), sem("y_done"), sem("yT_full"), sem("fin_done")
        stored = sem("stored")
        STACK = 16 * 4 * TERMS

        def program(eng, step):
            for i in range(-2, LOOP0):
                step(Batch(0, i))
            with eng.Fori(0, (LOOP1 - LOOP0) // NBUF) as k:
                for r in range(NBUF):
                    step(Batch(k, LOOP0 + r))
            for i in range(LOOP1, B + 1):
                step(Batch(0, i))

        def tokens(t, b):
            return t[b.n].rearrange("(t p) d -> p t d", p=128)

        block = ctx.enter_context(nc.Block())

        @block.sync
        def _(sp):
            sp.dma_start(x_nat[0][:, :, :], x[0].rearrange("(t p) d -> p t d", p=128)).then_inc(x_in[0], 16)
            sp.dma_start(wq_nat[:, :], wq.rearrange("d h e -> d (h e)")).then_inc(w_qk, 16)
            sp.dma_start(wk_nat[:, :], wk.rearrange("d h e -> d (h e)")).then_inc(w_qk, 16)
            sp.dma_start(wg_int[:, :, :], wg.rearrange("(c p) d -> p c d", p=128)).then_inc(w_ffn, 16)
            sp.dma_start(wu_int[:, :, :], wu.rearrange("(c p) d -> p c d", p=128)).then_inc(w_ffn, 16)
            sp.dma_start(wd_int[:, :], wd[:, :]).then_inc(w_ffn, 16)
            sp.dma_start(wv_sb[:, :], wv.rearrange("d h e -> d (h e)")).then_inc(w_vo, 16)
            sp.dma_start(x_nat[1][:, :, :], x[1].rearrange("(t p) d -> p t d", p=128)).then_inc(x_in[1], 16)
            sp.dma_start(wo_nat[:, :], wout.rearrange("h e d -> (h e) d")).then_inc(w_vo, 16)

            def spread(parts, stack, part_of, part, b):
                for side in range(2):
                    for term in range(TERMS):
                        if part_of[term] != part:
                            continue
                        row = 64 * side + E * term
                        sp.dma_start(stack[b.buf][row:row + E, :, :],
                                     parts[64 * side:64 * side + 64, part, :]).then_inc(stack_in, 16)

            def send_max(b, half):
                sp.wait_ge(mT_out, alone(sp, consts, b.count(2, half + 1)))
                pitch = SL * L
                for part in range(2):
                    dst = bass.AP(q_stack[b.buf], (KQ + part) * pitch + 4 * half * L,
                                  [[64 * pitch, 2], [L, 4], [1, L]])
                    sp.dma_start(dst, mT_sb[8 * part:8 * part + 8, half, :]).then_inc(m_in[half], 16)

            def send_o(b, half):
                sp.wait_ge(ov_out, alone(sp, consts, b.count(2, half + 1)))
                if b.after(1):
                    sp.wait_ge(on_ready, alone(sp, consts, b.count(1, 0)))
                rows = slice(64 * half, 64 * half + 64)
                sp.dma_start(sums[rows, :], o_ev[1::E, half, :]).then_inc(o_in[half], 16)
                sp.dma_start(o_sb[rows, :], o_ev[0::2, half, :]).then_inc(o_in[half], 16)

            def ones_rows():
                sp.wait_ge(consts, 1)
                pitch = SL * L
                for n in range(NBUF):
                    for part in range(2):
                        dst = bass.AP(k_stack[n], (KQ + part) * pitch, [[64 * pitch, 2], [128, SL * L // 128], [1, 128]])
                        sp.dma_start(dst, ones[:, :]).then_inc(ones_in, 16)

            def step(i):
                fe, ff, tail = i.at(2), i.at(1), i.at(-1)
                if fe.real and fe.after(2):
                    if fe.after(3):
                        sp.wait_ge(xhat_ready, alone(sp, consts, fe.at(-2).count(1, 0)))
                    sp.dma_start(x_nat[fe.buf][:, :, :], tokens(x, fe)).then_inc(x_in[fe.buf], 16)
                if i.real:
                    send_max(i, 1)
                if i.real:
                    sp.dma_start(x_res[i.buf][:, :, :], tokens(x, i)).then_inc(xr_in[i.buf], 16)
                if tail.real:
                    send_o(tail, 1)
                if fe.real:
                    if fe.after(3):
                        sp.wait_ge(s2_full, alone(sp, consts, fe.at(-2).count(U2, 0)))
                    sp.wait_ge(q_hi, alone(sp, consts, fe.count(1, 1)))
                    spread(q_parts, q_stack, Q_PART, 0, fe)
                    sp.wait_ge(k_hi, alone(sp, consts, fe.count(1, 1)))
                    spread(k_parts, k_stack, K_PART, 0, fe)
                if tail.real:
                    sp.wait_ge(rsum_done, alone(sp, consts, tail.count(1, 1)))
                    for e in range(T):
                        sp.dma_start(rden[e::T, :], rsums[:, :]).then_inc(rden_in, 16)
                if fe.real:
                    sp.wait_ge(q_mid, alone(sp, consts, fe.count(1, 1)))
                    spread(q_parts, q_stack, Q_PART, 1, fe)
                    sp.wait_ge(k_mid, alone(sp, consts, fe.count(1, 1)))
                    spread(k_parts, k_stack, K_PART, 1, fe)
                    sp.wait_ge(q_lo, alone(sp, consts, fe.count(1, 1)))
                    spread(q_parts, q_stack, Q_PART, 2, fe)
                    sp.wait_ge(k_lo, alone(sp, consts, fe.count(1, 1)))
                    spread(k_parts, k_stack, K_PART, 2, fe)
                if ff.real:
                    send_max(ff, 0)
                if i.real:
                    send_o(i, 0)
                if i.first:
                    ones_rows()

            program(sp, step)
            sp.wait_ge(stored, 16 * B)

        @block.gpsimd
        def _(pool):
            nc.gpsimd.memset(ident[:, :], 1.0)
            nc.gpsimd.memset(causal[:, :], 0.0).then_inc(w_conv, 1)
            pool.wait_ge(w_conv, 1)
            nc.gpsimd.affine_select(out=ident[:, :], in_=ident[:, :], compare_op=ALU.is_equal, fill=0.0,
                                    base=0, pattern=[[1, 128]], channel_multiplier=-1).then_inc(w_conv, 1)
            diag = causal[:, L - 128:]
            nc.gpsimd.affine_select(out=diag, in_=diag, compare_op=ALU.is_ge, fill=MASKED,
                                    base=0, pattern=[[-1, 128]], channel_multiplier=1).then_inc(w_conv, 1)

            def rsqrt(b):
                pool.wait_ge(ln_stats, alone(pool, consts, b.count(2, 2)))
                if b.after(1):
                    pool.wait_ge(xhat_ready, alone(pool, consts, b.count(1, 0)))
                nc.gpsimd.tensor_scalar(var_e[:, :], moments[:, :, 1], EPS, None, ALU.add).then_inc(newton, 1)
                pool.wait_ge(newton, alone(pool, consts, b.count(NEWTON, 1)))
                nc.gpsimd.tensor_scalar(rstd[:, :].bitcast(I32), var_e[:, :].bitcast(I32),
                                        -0.5, float(0x5F3759DF), ALU.mult, ALU.add).then_inc(newton, 1)
                for n in range(3):
                    pool.wait_ge(newton, alone(pool, consts, b.count(NEWTON, 4 * n + 2)))
                    nc.gpsimd.tensor_tensor(newt[:, :], rstd[:, :], rstd[:, :], ALU.mult).then_inc(newton, 1)
                    pool.wait_ge(newton, alone(pool, consts, b.count(NEWTON, 4 * n + 3)))
                    nc.gpsimd.tensor_tensor(newt[:, :], newt[:, :], var_e[:, :], ALU.mult).then_inc(newton, 1)
                    pool.wait_ge(newton, alone(pool, consts, b.count(NEWTON, 4 * n + 4)))
                    nc.gpsimd.tensor_scalar(newt[:, :], newt[:, :], -0.5, 1.5,
                                            ALU.mult, ALU.add).then_inc(newton, 1)
                    pool.wait_ge(newton, alone(pool, consts, b.count(NEWTON, 4 * n + 5)))
                    nc.gpsimd.tensor_tensor(rstd[:, :], rstd[:, :], newt[:, :], ALU.mult).then_inc(newton, 1)

            def mask(b, slot):
                g, r = divmod(slot, 5)
                pool.wait_ge(exp_done, alone(pool, consts, b.count(U2, 2 * slot + 2)))
                pair = probs[g % 2][:, 2 * r:2 * r + 2, :].rearrange("p u (n c) -> p u n c", c=128)
                if r < 2:
                    parts = [pair[:, :, 0, :]]
                elif r < 4:
                    parts = [pair[:, 0, 0::3, :], pair[:, 1, 0::3, :]]
                else:
                    parts = [pair[:, :, :, :].rearrange("p u n c -> p (u n) c")[:, 0::2, :]]
                for part in parts:
                    nc.gpsimd.affine_select(out=part, in_=part, compare_op=ALU.is_ge, fill=0.0, base=0,
                                            pattern=[[0, part.shape[1]], [1, 128]],
                                            channel_multiplier=-1).then_inc(masked, 1)

            def v_constants():
                for n in range(NBUF):
                    last = nc.gpsimd.memset(v_cols[n][:, :, :, :, :, :].rearrange("p t f s c m -> p (t f s c m)"), 0.0)
                last.then_inc(v_set, 1)
                pool.wait_ge(v_set, 1)
                for n in range(NBUF):
                    cols = v_cols[n][:, :, :, :, :, :].rearrange("p t f s c m -> p (t f) s c m")
                    nc.gpsimd.memset(cols[:, :, 0, :, 1:2 * E:2], 1.0)
                    last = nc.gpsimd.memset(cols[:, :, 1, :, 2 * E + 1:4 * E:2], 1.0)
                last.then_inc(v_set, 1)

            def step(i):
                fe, ff, tail = i.at(2), i.at(1), i.at(-1)
                for slot in range(SLOTS):
                    if slot == 1 and fe.real:
                        rsqrt(fe)
                    if slot in UP_READ and ff.real:
                        c = UP_READ.index(slot)
                        pool.wait_ge(gs_done, alone(pool, consts, ff.count(HC, c + 1)))
                        pool.wait_ge(up_out, alone(pool, consts, ff.count(HC, c + 1)))
                        nc.gpsimd.tensor_tensor(hT[:, c, :], hT[:, c, :], gate_s[:, c, :], ALU.mult).then_inc(h_done, 1)
                    if slot == 9 and fe.real:
                        pool.wait_ge(q_f, alone(pool, consts, fe.count(1, 1)))
                        nc.gpsimd.tensor_tensor(q_rest[:, :], q_rest[:, :], q_parts[:, 0, :],
                                                ALU.subtract).then_inc(q_r1, 1)
                    if slot == 10 and fe.real:
                        pool.wait_ge(k_f, alone(pool, consts, fe.count(1, 1)))
                        nc.gpsimd.tensor_tensor(k_rest[:, :], k_rest[:, :], k_parts[:, 0, :],
                                                ALU.subtract).then_inc(k_r1, 1)
                    if slot == 11 and fe.real:
                        pool.wait_ge(q_mid, alone(pool, consts, fe.count(1, 1)))
                        nc.gpsimd.tensor_tensor(q_parts[:, 2, :], q_rest[:, :], q_parts[:, 1, :],
                                                ALU.subtract).then_inc(q_lo, 1)
                    if slot == 12 and fe.real:
                        pool.wait_ge(k_mid, alone(pool, consts, fe.count(1, 1)))
                        nc.gpsimd.tensor_tensor(k_parts[:, 2, :], k_rest[:, :], k_parts[:, 1, :],
                                                ALU.subtract).then_inc(k_lo, 1)
                    if slot == 13 and i.second:
                        v_constants()
                    if i.real:
                        mask(i, slot)

            program(pool, step)

        @block.scalar
        def _(act):
            def copy(dst, src):
                return nc.scalar.activation(dst, src, ACT.Copy)

            def ffn_weights_out():
                for n, (dst, src) in enumerate(((wgT, ov), (wuT, s2[0]), (wdT, s2[1]))):
                    act.wait_ge(w_tr, n + 1)
                    copy(dst[:, :, :].rearrange("p c m -> p (c m)"), src[:, 0:HID]).then_inc(w_ready, 1)

            def exp_unit(b, slot, n):
                g, r = divmod(slot, 5)
                u = 2 * slot + n
                if r == 0 and n == 0:
                    if b.after(1) or g > 1:
                        act.wait_ge(pv_done, b.count(16, 4 * (g - 1)))
                act.wait_ge(s2_full, b.count(U2, u + 1))
                nc.scalar.activation(probs[g % 2][:, 2 * r + 1 - n, :], s2[(U2 * b.off + u) % RING2][:, :],
                                     ACT.Exp, scale=float(E) ** -0.5).then_inc(exp_done, 1)

            def step(i):
                fe, ff, tail = i.at(2), i.at(1), i.at(-1)
                for scores, slot in slots_of(i):
                    if slot == 3 and i.real:
                        max_out(i, 1)
                    if scores == 12 and ff.real:
                        max_out(ff, 0)
                    if slot == 10 and i.first:
                        ffn_weights_out()
                    if slot in GATE_READ and ff.real:
                        c = GATE_READ.index(slot)
                        if ff.after(1) or c > 0:
                            act.wait_ge(gs_done, ff.count(HC, c))
                        act.wait_ge(gate_full, ff.count(HC, c + 1))
                        nc.scalar.activation(tanh_g[:, :], (mb_a, mb_b, mb_a)[c][:, :], ACT.Tanh,
                                             scale=0.5).then_inc(tanh_done, 1)
                    if slot == 6 and fe.real:
                        if fe.after(3):
                            act.wait_ge(v_full, fe.at(-2).count(1, 0))
                        act.wait_ge(xT_full, fe.count(1, 1))
                        copy(xT[fe.buf][:, :], mb_b[:, :]).then_inc(xT_out, 1)
                    if slot in UP_READ and ff.real:
                        c = UP_READ.index(slot)
                        if ff.after(1):
                            act.wait_ge(down_full, ff.count(1, 0))
                        act.wait_ge(up_full, ff.count(HC, c + 1))
                        copy(hT[:, c, :], (mb_b, mb_a, mb_b)[c][:, :]).then_inc(up_out, 1)
                    if slot == 8 and fe.real:
                        if fe.after(1):
                            act.wait_ge(stack_in, fe.count(STACK, 0))
                        act.wait_ge(q_full, fe.count(1, 1))
                        copy(q_parts[:, 0, :], mb_a[:, :]).then_inc(q_hi, 1)
                        copy(q_rest[:, :], mb_a[:, :]).then_inc(q_f, 1)
                    if slot == 9 and fe.real:
                        act.wait_ge(k_full, fe.count(1, 1))
                        copy(k_parts[:, 0, :], mb_b[:, :]).then_inc(k_hi, 1)
                        copy(k_rest[:, :], mb_b[:, :]).then_inc(k_f, 1)
                    if slot == 10 and fe.real:
                        act.wait_ge(q_r1, fe.count(1, 1))
                        copy(q_parts[:, 1, :], q_rest[:, :]).then_inc(q_mid, 1)
                    if slot == 11 and fe.real:
                        act.wait_ge(k_r1, fe.count(1, 1))
                        copy(k_parts[:, 1, :], k_rest[:, :]).then_inc(k_mid, 1)
                    if slot == 15 and ff.real:
                        if ff.after(1):
                            act.wait_ge(g_done, ff.count(1, 0))
                        act.wait_ge(down_full, ff.count(1, 1))
                        nc.scalar.activation(tanh_f[:, :], mb_b[:, :], ACT.Tanh, scale=0.5).then_inc(tf_done, 1)
                    if slot == 0 and i.real:
                        if i.off < LOOP0 and not i.looped:
                            act.wait_ge(v_set, 2)
                        act.wait_ge(v_full, i.count(1, 1))
                        dst = v_cols[i.buf][:, :, :, :, :, :].rearrange("p t f s c m -> p (t f) s c m")
                        src = mb_b[:, :].rearrange("p (g c s e) -> p g s c e", c=4, s=2, e=E)
                        copy(dst[:, :, 0, :, 0:2 * E:2], src[:, :, 0])
                        copy(dst[:, :, 1, :, 2 * E:4 * E:2], src[:, :, 1]).then_inc(v_out, 1)
                    if slot == 5 and tail.real:
                        heads_out(tail, 1)
                    if slot == 15 and i.real:
                        heads_out(i, 0)
                    if i.real:
                        exp_unit(i, slot, 0)
                        exp_unit(i, slot, 1)
                    if slot == 19 and tail.real:
                        act.wait_ge(fin_done, tail.count(1, 1))
                        act.dma_start(tokens(out, tail),
                                      y_sb[tail.buf][:, :].rearrange("p (t d) -> p t d", t=T)).then_inc(stored, 16)

            def max_out(b, half):
                if b.after(1):
                    act.wait_ge(m_in[half], b.count(32, 0))
                act.wait_ge(mT_full, b.count(2, half + 1))
                copy(mT_sb[:, half, :], mb_a[0:16, :]).then_inc(mT_out, 1)

            def heads_out(b, half):
                if b.after(1):
                    act.wait_ge(o_in[half], b.count(32, 0))
                act.wait_ge(pv_done, b.count(16, 8 * half + 8))
                copy(o_ev[:, half, :], ov[:, :]).then_inc(ov_out, 1)

            program(act, step)

        @block.vector
        def _(dve):
            nc.vector.memset(ones[:, :], 1.0).then_inc(consts, 1)
            dve.wait_ge(w_conv, 3)
            nc.vector.tensor_copy(ident_b[:, :], ident[:, :]).then_inc(consts, 1)

            def qk_weights():
                dve.wait_ge(w_qk, 32)
                for nat, dst in ((wq_nat, wq_sb), (wk_nat, wk_sb)):
                    src = nat[:, :].rearrange("p (f d a s e) -> p f a e s d", f=2, d=2, a=2, s=2)
                    to = dst[:, :].rearrange("p (a e f s d) -> p f a e s d", a=2, e=E, f=2, s=2)
                    for f in range(2):
                        for a in range(2):
                            last = nc.vector.tensor_copy(to[:, f, a], src[:, f, a])
                last.then_inc(w_float, 1)

            def other_weights():
                dve.wait_ge(w_ffn, 48)
                nc.vector.tensor_scalar(wg_f[:, :, :], wg_int[:, :, :], SCALE, None, ALU.mult)
                nc.vector.tensor_scalar(wu_f[:, :, :], wu_int[:, :, :], SCALE, None, ALU.mult)
                nc.vector.tensor_scalar(wd_f[:, :], wd_int[:, :], SCALE, 0.5, ALU.mult, ALU.mult)
                dve.wait_ge(w_vo, 32)
                nc.vector.tensor_scalar(wo_sb[:, :], wo_nat[:, :], 0.5, None, ALU.mult).then_inc(w_float, 1)

            def reduce_unit(b, u):
                tile, slots, side = P1_UNITS[u]
                half, width = u // (U1 // 2), 128 * (tile + 1)
                dve.wait_ge(s1_full, alone(dve, consts, b.count(U1, u + 1)))
                bank = s1[(U1 * b.off + u) % RING1]
                for n, s in enumerate(slots):
                    at = s - 4 * half
                    scores = bank[:, n * width:(n + 1) * width]
                    last = nc.vector.tensor_tensor_reduce(scores, scores, causal[:, L - width:], 1.0, MASKED,
                                                          ALU.add, ALU.max, rowmax[:, half, tile, side, at:at + 1])
                last.then_inc(s1_red, 1)

            def split_max(b, half):
                if b.after(1):
                    dve.wait_ge(mT_full, b.at(-1).count(2, half + 1))
                dve.wait_ge(s1_red, b.count(U1, U1 // 2 * (half + 1)))
                src = rowmax[:, half].rearrange("p t a s -> p t (a s)")
                nc.vector.tensor_scalar(negmax_p[:, half, :, 0, :], src, -1.0, None, ALU.mult).then_inc(nm_ready, 1)
                dve.wait_ge(nm_ready, b.count(4, 2 * half + 1))
                nc.vector.scalar_tensor_tensor(negmax_p[:, half, :, 1, :], src, -1.0, negmax_p[:, half, :, 0, :],
                                               ALU.mult, ALU.subtract).then_inc(nm_ready, 1)

            def step(i):
                fe, ff, tail = i.at(2), i.at(1), i.at(-1)
                for scores, slot in slots_of(i):
                    if ff.real and scores is not None:
                        reduce_unit(ff, P1_SLOT[scores][0])
                    if slot == 0 and fe.real:
                        dve.wait_ge(x_in[fe.buf], fe.turns(1))
                        for t in range(T):
                            last = nc.vector.bn_stats(stats[:, t, :], x_nat[fe.buf][:, t, :])
                        last.then_inc(ln_stats, 1)
                    if slot == 1 and fe.real:
                        if fe.after(1):
                            dve.wait_ge(xhat_ready, fe.count(1, 0))
                        dve.wait_ge(ln_stats, alone(dve, consts, fe.count(2, 1)))
                        for t in range(T):
                            last = nc.vector.bn_aggr(moments[:, t, :], stats[:, t, :])
                        last.then_inc(ln_stats, 1)
                    if slot == 1 and i.first:
                        qk_weights()
                    if slot == 10 and i.first:
                        other_weights()
                    if slot in GATE_READ and ff.real:
                        c = GATE_READ.index(slot)
                        if ff.after(1):
                            dve.wait_ge(h_done, ff.count(HC, c + 1 - HC))
                        dve.wait_ge(tanh_done, ff.count(HC, c + 1))
                        nc.vector.scalar_tensor_tensor(gate_s[:, c, :], tanh_g[:, :], 1.0, (mb_a, mb_b, mb_a)[c][:, :],
                                                       ALU.add, ALU.mult).then_inc(gs_done, 1)
                    if slot == 8 and tail.real:
                        if tail.after(1):
                            dve.wait_ge(rden_in, tail.count(16 * T, 0))
                        dve.wait_ge(o_in[0], tail.count(32, 32))
                        dve.wait_ge(o_in[1], tail.count(32, 32))
                        nc.vector.reciprocal(rsums[:, :], sums[:, :]).then_inc(rsum_done, 1)
                    if slot == 13 and tail.real:
                        if tail.after(1):
                            dve.wait_ge(out_full, tail.count(1, 0))
                        dve.wait_ge(rden_in, tail.count(16 * T, 16 * T))
                        nc.vector.tensor_tensor(o_norm[:, :], o_sb[:, :], rden[:, :], ALU.mult).then_inc(on_ready, 1)
                    if slot == 15 and ff.real:
                        dve.wait_ge(tf_done, ff.count(1, 1))
                        if ff.after(3):
                            dve.wait_ge(y_done, ff.at(-2).count(1, 0))
                        nc.vector.scalar_tensor_tensor(g_out[ff.buf][:, :], tanh_f[:, :], 1.0, mb_b[:, :],
                                                       ALU.add, ALU.mult).then_inc(g_done, 1)
                    if slot == 16 and tail.real:
                        if tail.after(1):
                            dve.wait_ge(yT_full, tail.count(1, 0))
                        dve.wait_ge(g_done, tail.count(1, 1))
                        dve.wait_ge(out_full, tail.count(1, 1))
                        nc.vector.tensor_tensor(sg[:, :], g_out[tail.buf][:, :], mb_a[:, :],
                                                ALU.mult).then_inc(y_done, 1)
                    if slot == 18 and tail.real:
                        if tail.after(1):
                            dve.wait_ge(stored, tail.count(16, 0))
                        dve.wait_ge(xr_in[tail.buf], tail.turns(1))
                        dve.wait_ge(yT_full, tail.count(1, 1))
                        nc.vector.tensor_tensor(y_sb[tail.buf][:, :], mb_a[:, :],
                                                x_res[tail.buf][:, :, :].rearrange("p t d -> p (t d)"),
                                                ALU.add).then_inc(fin_done, 1)
                    if ff.real and scores is not None:
                        for u in P1_SLOT[scores][1:]:
                            reduce_unit(ff, u)
                        if scores == 9:
                            split_max(ff, 0)
                        if scores == 19:
                            split_max(ff, 1)
                    if slot == 3 and fe.real:
                        if fe.after(1):
                            dve.wait_ge(xT_full, fe.count(1, 0))
                        dve.wait_ge(newton, fe.count(NEWTON, NEWTON))
                        for t in range(T):
                            last = nc.vector.tensor_scalar(x_hat[:, t, :], x_nat[fe.buf][:, t, :],
                                                           moments[:, t, 0:1], rstd[:, t:t + 1],
                                                           ALU.subtract, ALU.mult)
                        last.then_inc(xhat_ready, 1)

            program(dve, step)

        @block.tensor
        def _(pe):
            mm = nc.tensor.matmul

            def ffn_weights():
                pe.wait_ge(w_float, 2)
                for w, bank in ((wg_f, ov), (wu_f, s2[0])):
                    for c in range(HC):
                        last = nc.tensor.transpose(bank[:, 128 * c:128 * c + 128], w[:, c, :], ident[:, :])
                    last.then_inc(w_tr, 1)
                for c in range(HC):
                    last = nc.tensor.transpose(s2[1][:, 128 * c:128 * c + 128],
                                               wd_f[:, 128 * c:128 * c + 128], ident[:, :])
                last.then_inc(w_tr, 1)
                pe.wait_ge(w_ready, 3)

            def pass1(b, u):
                tile, slots, side = P1_UNITS[u]
                width = 128 * (tile + 1)
                rows = slice(64 * side, 64 * side + KQ)
                if u == 0:
                    pe.wait_ge(stack_in, b.count(STACK, STACK))
                if b.after(1) or u >= RING1:
                    pe.wait_ge(s1_red, b.count(U1, u + 1 - RING1))
                for n, s in enumerate(slots):
                    last = mm(s1[(U1 * b.off + u) % RING1][:, n * width:(n + 1) * width],
                              q_stack[b.buf][rows, s, 128 * tile:128 * tile + 128],
                              k_stack[b.buf][rows, s, 0:width], start=True, stop=True)
                last.then_inc(s1_full, 1)

            def pass2(b, slot, n):
                g, r = divmod(slot, 5)
                side, u = 1 - n, 2 * slot + n
                rows = slice(64 * side, 64 * side + KM)
                if u == 0 and not b.looped and b.off < LOOP0:
                    pe.wait_ge(ones_in, 16 * 2 * NBUF)
                if u in (0, U2 // 2):
                    pe.wait_ge(m_in[2 * u // U2], b.count(32, 32))
                if b.after(1) or u >= RING2:
                    pe.wait_ge(exp_done, b.count(U2, u + 1 - RING2))
                jobs = {0: [(2 * g, 0, 0)], 1: [(2 * g + 1, 0, 0)],
                        2: [(2 * g, 1, 0), (2 * g, 3, 384)], 3: [(2 * g + 1, 1, 0), (2 * g + 1, 3, 384)],
                        4: [(2 * g, 2, 0), (2 * g + 1, 2, 256)]}[r]
                for s, j, col in jobs:
                    last = mm(s2[(U2 * b.off + u) % RING2][:, col:col + L - 128 * j],
                              k_stack[b.buf][rows, s, 128 * j:128 * j + 128],
                              q_stack[b.buf][rows, s, 128 * j:L], start=True, stop=True)
                last.then_inc(s2_full, 1)

            def attend(b, g, j):
                half, sub = divmod(g, 2)
                if g == 0 and j == 0:
                    pe.wait_ge(v_out, b.count(1, 1))
                if sub == 0 and j == 0:
                    if b.after(1) or half > 0:
                        pe.wait_ge(ov_out, b.count(2, half))
                pe.wait_ge(masked, b.count(28, 7 * g + (2, 6, 7, 7)[j]))
                for c in range(4):
                    side, d = c % 2, c // 2
                    unit, col = {0: (d, 0), 1: (2 + d, 0), 2: (4, 256 * d), 3: (2 + d, 384)}[j]
                    last = mm(ov[32 * c:32 * c + 32, 128 * j:L], v_cols[b.buf][:, j, half, sub, c, :],
                              probs[g % 2][:, 2 * unit + side, col:col + L - 128 * j],
                              start=sub == 0 and j == 0, stop=sub == 1 and j == 3, skip_group_check=True)
                last.then_inc(pv_done, 1)

            def max_T(b, half):
                pe.wait_ge(nm_ready, b.count(4, 2 * half + 2))
                for t in range(T):
                    last = mm(mb_a[0:16, 128 * t:128 * t + 128],
                              negmax_p[:, half, t].rearrange("p a h -> p (a h)"), ident_b[:, :], start=True, stop=True)
                last.then_inc(mT_full, 1)

            def step(i):
                fe, ff, tail = i.at(2), i.at(1), i.at(-1)
                for scores, slot in slots_of(i):
                    for n in range(2):
                        if ff.real and scores is not None:
                            pass1(ff, P1_SLOT[scores][n])
                        if i.real:
                            pass2(i, scores, n)
                    if ff.real and scores is not None and len(P1_SLOT[scores]) == 3:
                        pass1(ff, P1_SLOT[scores][2])
                    if slot in GATE_MADE and ff.real:
                        c = GATE_MADE.index(slot)
                        if c == 0:
                            if i.after(2):
                                pe.wait_ge(fin_done, i.at(-1).count(1, 0))
                            elif i.real:
                                pe.wait_ge(mT_out, i.count(2, 1))
                            else:
                                pe.wait_ge(q_f, ff.count(1, 1))
                        elif c == 1:
                            pe.wait_ge(up_out, ff.count(HC, 1))
                        elif fe.real:
                            pe.wait_ge(q_f, fe.count(1, 1))
                        else:
                            pe.wait_ge(up_out, ff.count(HC, 2))
                        mm((mb_a, mb_b, mb_a)[c][:, :], wgT[:, c, :], xT[ff.buf][:, :],
                           start=True, stop=True).then_inc(gate_full, 1)
                    if slot in UP_MADE and ff.real:
                        c = UP_MADE.index(slot)
                        if c == 0:
                            if i.real:
                                pe.wait_ge(v_out, i.count(1, 1))
                            else:
                                pe.wait_ge(k_f, ff.count(1, 1))
                        elif c == 1:
                            if i.real:
                                pe.wait_ge(mT_out, i.count(2, 2))
                            else:
                                pe.wait_ge(gs_done, ff.count(HC, 1))
                        elif fe.real:
                            pe.wait_ge(k_f, fe.count(1, 1))
                        else:
                            pe.wait_ge(gs_done, ff.count(HC, 2))
                        mm((mb_b, mb_a, mb_b)[c][:, :], wuT[:, c, :], xT[ff.buf][:, :],
                           start=True, stop=True).then_inc(up_full, 1)
                    if slot == 2 and i.real:
                        if ff.real:
                            pe.wait_ge(gs_done, ff.count(HC, 1))
                        else:
                            pe.wait_ge(fin_done, i.at(-1).count(1, 0))
                        max_T(i, 1)
                    if slot == 5 and fe.real:
                        if ff.real:
                            pe.wait_ge(gs_done, ff.count(HC, 2))
                        else:
                            pe.wait_ge(w_conv, 2)
                        pe.wait_ge(xhat_ready, fe.count(1, 1))
                        for t in range(T):
                            last = nc.tensor.transpose(mb_b[:, 128 * t:128 * t + 128], x_hat[:, t, :], ident[:, :])
                        last.then_inc(xT_full, 1)
                    if slot == 7 and fe.real:
                        if i.first:
                            pe.wait_ge(w_float, 1)
                        if ff.real:
                            pe.wait_ge(up_out, ff.count(HC, 2))
                        pe.wait_ge(xT_out, fe.count(1, 1))
                        mm(mb_a[:, :], wq_sb[:, :], xT[fe.buf][:, :], start=True, stop=True).then_inc(q_full, 1)
                    if slot == 8 and fe.real:
                        mm(mb_b[:, :], wk_sb[:, :], xT[fe.buf][:, :], start=True, stop=True).then_inc(k_full, 1)
                    if slot == 10 and i.first:
                        ffn_weights()
                        pe.wait_ge(consts, 2)
                        pe.wait_ge(w_vo, 32)
                    if scores == 11 and ff.real:
                        pe.wait_ge(gs_done, ff.count(HC, HC))
                        max_T(ff, 0)
                    if slot in DOWN_MADE and ff.real:
                        c = DOWN_MADE.index(slot)
                        if c == 0:
                            pe.wait_ge(up_out, ff.count(HC, HC))
                        pe.wait_ge(h_done, ff.count(HC, c + 1))
                        last = mm(mb_b[:, :], wdT[:, c, :], hT[:, c, :], start=c == 0, stop=c == HC - 1)
                        if c == HC - 1:
                            last.then_inc(down_full, 1)
                    if slot == 15 and tail.real:
                        if ff.real:
                            pe.wait_ge(mT_out, ff.count(2, 1))
                        elif i.real:
                            pe.wait_ge(mT_out, i.count(2, 2))
                        else:
                            pe.wait_ge(fin_done, tail.count(1, 0))
                        pe.wait_ge(on_ready, tail.count(1, 1))
                        mm(mb_a[:, :], wo_sb[:, :], o_norm[:, :], start=True, stop=True).then_inc(out_full, 1)
                    if slot == 17 and tail.real:
                        pe.wait_ge(y_done, tail.count(1, 1))
                        for t in range(T):
                            last = nc.tensor.transpose(mb_a[:, 128 * t:128 * t + 128],
                                                       sg[:, 128 * t:128 * t + 128], ident[:, :])
                        last.then_inc(yT_full, 1)
                    if slot == 19 and ff.real:
                        pe.wait_ge(g_done, ff.count(1, 1))
                        for t in range(T):
                            last = mm(mb_b[:, 128 * t:128 * t + 128], xT[ff.buf][:, 128 * t:128 * t + 128],
                                      wv_sb[:, :], start=True, stop=True)
                        last.then_inc(v_full, 1)
                    if slot in PV_SLOT:
                        g, j = PV_SLOT[slot]
                        b = tail if g == 3 else i
                        if b.real:
                            attend(b, g, j)

            program(pe, step)


_INS = ["L0_attn_x", "L0_attn_Wq", "L0_attn_Wk", "L0_attn_Wv", "L0_attn_Wout",
        "L0_ffn_w_gate", "L0_ffn_w_up", "L0_ffn_w_down"]


def kernel(**inputs):
    import concourse.bacc as _bacc
    import numpy as _np
    from concourse import mybir as _mybir
    from concourse.bass_utils import run_bass_kernel_spmd as _run

    nc = _bacc.Bacc("TRN2", target_bir_lowering=False, num_devices=1)
    arrays, args = {}, []
    for name in _INS:
        a = _np.ascontiguousarray(inputs[name])
        arrays[f"in_{name}"] = a
        args.append(nc.dram_tensor(f"in_{name}", a.shape, _mybir.dt.from_np(a.dtype), kind="ExternalInput").ap())
    args.append(nc.dram_tensor("y", (B, L, D), _mybir.dt.float32, kind="ExternalOutput").ap())
    build(nc, *args)
    r = _run(nc, [arrays], core_ids=[0])
    return r.results[0]["y"]
```
